# Optimizing a Trainium2 kernel written in Bass

```python
import numpy as np
import jax
import jax.numpy as jnp

def _softmax(x, axis=-1):
    return jax.nn.softmax(x, axis=axis)

def _gelu(x):
    return jax.nn.gelu(x, approximate=True)

def _silu(x):
    return jax.nn.silu(x)

def _sigmoid(x):
    return jax.nn.sigmoid(x)

def _layernorm(x, axis=-1, eps=1e-05):
    m = jnp.mean(x, axis=axis, keepdims=True)
    v = jnp.var(x, axis=axis, keepdims=True)
    return (x - m) / jnp.sqrt(v + eps)

def _scatter_add(tgt, idx, src, axis=0):
    return tgt.at[idx].add(src)

def _segment_sum(src, seg, n):
    return jax.ops.segment_sum(src, seg, n)
kernel_name = 'mk_adj_preln_d4_adj_r2_645b92'

def setup_inputs(seed: int=0):
    np.random.seed(seed)
    _w = jnp.asarray

    def _rec_inputs():
        import jax
        import jax.numpy as jnp
        _gk = jax.random.key(seed)
        x = 7.22e-05 + 1 * jax.random.normal(jax.random.fold_in(_gk, 1), (64, 128, 128), jnp.float32)
        _a = jax.random.bernoulli(jax.random.fold_in(_gk, 2), 0.03125, (64, 128, 128))
        _a = jnp.logical_or(_a, jnp.eye(128, dtype=bool))
        _af = _a.astype(jnp.float32)
        _af = _af * jax.random.uniform(jax.random.fold_in(_gk, 3), (64, 128, 128), jnp.float32, 0.05, 1)
        adj = _af
        return (x, adj)
    x, adj = _rec_inputs()

    def _L0_gnn_setup():
        import jax, jax.numpy as jnp
        import numpy as np
        T, N, D = (8, 2048, 128)
        NUM_LAYERS = 1
        key = jax.random.key(seed)
        ks = jax.random.split(key, 8)
        s = 1.0 / np.sqrt(D)
        return {'x_seq': jax.random.normal(ks[0], (T, N, D), jnp.float32), 'A_seq': jax.random.uniform(ks[1], (T, N, N), jnp.float32), 'pool_p': jax.random.normal(ks[2], (D,), jnp.float32) * s, 'W_ih': jax.random.normal(ks[3], (3 * D, D), jnp.float32) * s, 'W_hh': jax.random.normal(ks[4], (3 * D, D), jnp.float32) * s, 'b_ih': jnp.zeros((3 * D,), jnp.float32), 'b_hh': jnp.zeros((3 * D,), jnp.float32), 'W0': jax.random.normal(ks[5], (NUM_LAYERS, D, D), jnp.float32) * s}
    _L0_gnn_all = _L0_gnn_setup()
    _L0_gnn_in = {k: v for k, v in _L0_gnn_all.items() if k in ('pool_p', 'W_ih', 'W_hh', 'b_ih', 'b_hh', 'W0')}
    del _L0_gnn_all

    def _L1_gnn_setup():
        import jax, jax.numpy as jnp
        import numpy as np
        B, N, D = (8, 256, 128)
        key = jax.random.key(seed)
        ks = jax.random.split(key, 10)
        s = 1.0 / np.sqrt(D)
        u = lambda k, shape: jax.random.uniform(k, shape, jnp.float32, -s, s)
        return {'h_e': jax.random.normal(ks[0], (B, N, D), jnp.float32), 'adj': jax.random.uniform(ks[1], (B, N, N), jnp.float32), 'W_ioux': u(ks[2], (2 * D, D)), 'b_ioux': u(ks[3], (2 * D,)), 'W_iouh': u(ks[4], (2 * D, D)), 'b_iouh': u(ks[5], (2 * D,)), 'W_coux': u(ks[6], (D, D)), 'b_coux': u(ks[7], (D,)), 'W_couh': u(ks[8], (D, D)), 'b_couh': u(ks[9], (D,))}
    _L1_gnn_all = _L1_gnn_setup()
    _L1_gnn_in = {k: v for k, v in _L1_gnn_all.items() if k in ('W_ioux', 'b_ioux', 'W_iouh', 'b_iouh', 'W_coux', 'b_coux', 'W_couh', 'b_couh')}
    del _L1_gnn_all

    def _L2_gnn_setup():
        import jax, jax.numpy as jnp
        import numpy as np
        D_IN = 128
        D_HID = 256
        key = jax.random.key(seed)
        k1, k2, k3, k4, k5, k6 = jax.random.split(key, 6)
        x = jax.random.normal(k1, (8, 2048, D_IN), dtype=jnp.float32)
        adj = jax.random.uniform(k2, (8, 2048, 2048), dtype=jnp.float32)
        s1 = 1.0 / np.sqrt(D_IN)
        s2 = 1.0 / np.sqrt(D_HID)
        W1 = jax.random.uniform(k3, (D_IN, D_HID), dtype=jnp.float32, minval=-s1, maxval=s1)
        b1 = jax.random.uniform(k4, (D_HID,), dtype=jnp.float32, minval=-s1, maxval=s1)
        W2 = jax.random.uniform(k5, (D_HID, D_IN), dtype=jnp.float32, minval=-s2, maxval=s2)
        b2 = jax.random.uniform(k6, (D_IN,), dtype=jnp.float32, minval=-s2, maxval=s2)
        eps = jnp.zeros((1,), dtype=jnp.float32)
        return {'x': x, 'adj': adj, 'eps': eps, 'W1': W1, 'b1': b1, 'W2': W2, 'b2': b2}
    _L2_gnn_all = _L2_gnn_setup()
    _L2_gnn_in = {k: v for k, v in _L2_gnn_all.items() if k in ('eps', 'W1', 'b1', 'W2', 'b2')}
    del _L2_gnn_all

    def _L3_gnn_setup():
        import jax, jax.numpy as jnp
        import numpy as np
        B, K, H = (32, 512, 128)
        LN_EPS = 1e-05

        def layer_norm(x, gamma, beta):
            mu = jnp.mean(x, axis=-1, keepdims=True)
            var = jnp.mean(jnp.square(x - mu), axis=-1, keepdims=True)
            return (x - mu) * jax.lax.rsqrt(var + LN_EPS) * gamma + beta
        key = jax.random.key(seed)
        k1, k2, k3, k4 = jax.random.split(key, 4)
        x = jax.random.normal(k1, (B, K, H), dtype=jnp.float32)
        adj = jax.random.uniform(k2, (B, K, K), dtype=jnp.float32)
        s = 1.0 / np.sqrt(H)
        W_rel = jax.random.normal(k3, (H, H), dtype=jnp.float32) * s
        b_rel = jnp.zeros((H,), dtype=jnp.float32)
        W_root = jax.random.normal(k4, (H, H), dtype=jnp.float32) * s
        ln_gamma = jnp.ones((H,), dtype=jnp.float32)
        ln_beta = jnp.zeros((H,), dtype=jnp.float32)
        return {'x': x, 'adj': adj, 'W_rel': W_rel, 'b_rel': b_rel, 'W_root': W_root, 'ln_gamma': ln_gamma, 'ln_beta': ln_beta}
    _L3_gnn_all = _L3_gnn_setup()
    _L3_gnn_in = {k: v for k, v in _L3_gnn_all.items() if k in ('W_rel', 'b_rel', 'W_root', 'ln_gamma', 'ln_beta')}
    del _L3_gnn_all
    return {'x': x, 'adj': adj, 'L0_gnn_pool_p': _L0_gnn_in['pool_p'], 'L0_gnn_W_ih': _L0_gnn_in['W_ih'], 'L0_gnn_W_hh': _L0_gnn_in['W_hh'], 'L0_gnn_b_ih': _L0_gnn_in['b_ih'], 'L0_gnn_b_hh': _L0_gnn_in['b_hh'], 'L0_gnn_W0': _L0_gnn_in['W0'], 'L1_gnn_W_ioux': _L1_gnn_in['W_ioux'], 'L1_gnn_b_ioux': _L1_gnn_in['b_ioux'], 'L1_gnn_W_iouh': _L1_gnn_in['W_iouh'], 'L1_gnn_b_iouh': _L1_gnn_in['b_iouh'], 'L1_gnn_W_coux': _L1_gnn_in['W_coux'], 'L1_gnn_b_coux': _L1_gnn_in['b_coux'], 'L1_gnn_W_couh': _L1_gnn_in['W_couh'], 'L1_gnn_b_couh': _L1_gnn_in['b_couh'], 'L2_gnn_eps': _L2_gnn_in['eps'], 'L2_gnn_W1': _L2_gnn_in['W1'], 'L2_gnn_b1': _L2_gnn_in['b1'], 'L2_gnn_W2': _L2_gnn_in['W2'], 'L2_gnn_b2': _L2_gnn_in['b2'], 'L3_gnn_W_rel': _L3_gnn_in['W_rel'], 'L3_gnn_b_rel': _L3_gnn_in['b_rel'], 'L3_gnn_W_root': _L3_gnn_in['W_root'], 'L3_gnn_ln_gamma': _L3_gnn_in['ln_gamma'], 'L3_gnn_ln_beta': _L3_gnn_in['ln_beta']}

def reference(x, adj, L0_gnn_pool_p, L0_gnn_W_ih, L0_gnn_W_hh, L0_gnn_b_ih, L0_gnn_b_hh, L0_gnn_W0, L1_gnn_W_ioux, L1_gnn_b_ioux, L1_gnn_W_iouh, L1_gnn_b_iouh, L1_gnn_W_coux, L1_gnn_b_coux, L1_gnn_W_couh, L1_gnn_b_couh, L2_gnn_eps, L2_gnn_W1, L2_gnn_b1, L2_gnn_W2, L2_gnn_b2, L3_gnn_W_rel, L3_gnn_b_rel, L3_gnn_W_root, L3_gnn_ln_gamma, L3_gnn_ln_beta):
    import jax
    import jax.numpy as jnp

    def _L0_gnn_ref(x_seq, A_seq, pool_p, W_ih, W_hh, b_ih, b_hh, W0):
        import jax, jax.numpy as jnp
        import numpy as np
        T, N, D = (8, 2048, 128)
        NUM_LAYERS = 1
        k = W0.shape[-1]
        p_norm = jnp.linalg.norm(pool_p)

        def gru_cell(h, xin):
            gi = xin @ W_ih.T + b_ih
            gh = h @ W_hh.T + b_hh
            i_r, i_z, i_n = jnp.split(gi, 3, axis=-1)
            h_r, h_z, h_n = jnp.split(gh, 3, axis=-1)
            r = jax.nn.sigmoid(i_r + h_r)
            z = jax.nn.sigmoid(i_z + h_z)
            n = jnp.tanh(i_n + r * h_n)
            return (1.0 - z) * n + z * h

        def step(W, inp):
            x, A = inp
            score = x @ pool_p / p_norm
            vals, idx = jax.lax.top_k(score, k)
            x_hat = x[idx] * jnp.tanh(vals)[:, None]
            W_new = gru_cell(W[-1], x_hat)[None]
            out = A @ (x @ W_new[-1])
            return (W_new, out)
        _, outs = jax.lax.scan(step, W0, (x_seq, A_seq))
        return outs

    def _L1_gnn_ref(h_e, adj, W_ioux, b_ioux, W_iouh, b_iouh, W_coux, b_coux, W_couh, b_couh):
        import jax, jax.numpy as jnp
        import numpy as np
        B, N, D = (8, 256, 128)
        n = h_e.shape[1]
        d = jnp.sum(adj, axis=-1)
        dinv = jnp.where(d != 0, 1.0 / jnp.where(d != 0, d, 1.0), 0.0)
        norm_adjT = jnp.swapaxes(adj, 1, 2) * dinv[:, :, None]

        def step(h, i):
            x = jnp.take(h_e, i, axis=1)
            row = jnp.take(norm_adjT, i, axis=1)
            x_par = jnp.einsum('bj,bjd->bd', row, h)
            iou = x @ W_ioux.T + b_ioux + x_par @ W_iouh.T + b_iouh
            r, z = jnp.split(iou, 2, axis=1)
            r, z = (jax.nn.sigmoid(r), jax.nn.sigmoid(z))
            hc = jnp.tanh(x @ W_coux.T + b_coux + x_par * r @ W_couh.T + b_couh)
            h_new = z * x_par + (1.0 - z) * hc
            h = jax.lax.dynamic_update_slice(h, h_new[:, None, :], (0, i, 0))
            return (h, None)
        h_out, _ = jax.lax.scan(step, h_e, jnp.arange(n))
        return h_out

    def _L2_gnn_ref(x, adj, eps, W1, b1, W2, b2):
        import jax, jax.numpy as jnp
        import numpy as np
        D_IN = 128
        D_HID = 256
        aggregated = jnp.einsum('bnm,bmd->bnd', adj, x)
        h = (1.0 + eps) * x + aggregated
        h = jax.nn.relu(h @ W1 + b1)
        return h @ W2 + b2

    def _L3_gnn_ref(x, adj, W_rel, b_rel, W_root, ln_gamma, ln_beta):
        import jax, jax.numpy as jnp
        import numpy as np
        B, K, H = (32, 512, 128)
        LN_EPS = 1e-05

        def layer_norm(x, gamma, beta):
            mu = jnp.mean(x, axis=-1, keepdims=True)
            var = jnp.mean(jnp.square(x - mu), axis=-1, keepdims=True)
            return (x - mu) * jax.lax.rsqrt(var + LN_EPS) * gamma + beta
        h = layer_norm(x, ln_gamma, ln_beta)
        agg = jnp.einsum('bij,bjh->bih', adj, h)
        conv = jnp.einsum('bkh,ho->bko', agg, W_rel) + b_rel + jnp.einsum('bkh,ho->bko', h, W_root)
        return x + jax.nn.relu(conv)
    h = jnp.maximum(_layernorm(x, axis=-1), 0.0)
    x = x + _L0_gnn_ref(h, adj, L0_gnn_pool_p, L0_gnn_W_ih, L0_gnn_W_hh, L0_gnn_b_ih, L0_gnn_b_hh, L0_gnn_W0)
    h = jnp.maximum(_layernorm(x, axis=-1), 0.0)
    x = x + _L1_gnn_ref(h, adj, L1_gnn_W_ioux, L1_gnn_b_ioux, L1_gnn_W_iouh, L1_gnn_b_iouh, L1_gnn_W_coux, L1_gnn_b_coux, L1_gnn_W_couh, L1_gnn_b_couh)
    h = jnp.maximum(_layernorm(x, axis=-1), 0.0)
    x = x + _L2_gnn_ref(h, adj, L2_gnn_eps, L2_gnn_W1, L2_gnn_b1, L2_gnn_W2, L2_gnn_b2)
    h = jnp.maximum(_layernorm(x, axis=-1), 0.0)
    x = x + _L3_gnn_ref(h, adj, L3_gnn_W_rel, L3_gnn_b_rel, L3_gnn_W_root, L3_gnn_ln_gamma, L3_gnn_ln_beta)
    return x

_drawn_inputs = setup_inputs


def setup_inputs(seed=0):
    import zlib

    import numpy as np

    out = dict(_drawn_inputs(seed))
    spreads = {'L0_gnn_b_ih': (0.0, 0.1),
     'L0_gnn_b_hh': (0.0, 0.1),
     'L3_gnn_b_rel': (0.0, 2.0),
     'L3_gnn_ln_gamma': (1.0, 0.6),
     'L3_gnn_ln_beta': (0.0, 0.8)}
    factors = {'L0_gnn_W0': 8.0,
     'L1_gnn_W_ioux': 8.0,
     'L1_gnn_b_ioux': 64.0,
     'L1_gnn_b_iouh': 64.0,
     'L1_gnn_W_coux': 3.992,
     'L1_gnn_b_coux': 64.0,
     'L1_gnn_W_couh': 7.927,
     'L1_gnn_b_couh': 47.941,
     'L2_gnn_W1': 2.736,
     'L2_gnn_b1': 62.8,
     'L2_gnn_b2': 33.754}
    for name, (base, spread) in spreads.items():
        noise = np.random.default_rng([zlib.crc32(name.encode()), seed]).standard_normal(out[name].shape)
        drawn = base * np.exp(spread * noise) if base else spread * noise
        out[name] = jnp.asarray(drawn.astype(out[name].dtype))
    for name, factor in factors.items():
        out[name] = (out[name] * factor).astype(out[name].dtype)
    return out
```

```python
from contextlib import ExitStack

import concourse.bass as bass
from concourse import mybir

F32 = mybir.dt.float32
ALU = mybir.AluOpType
ACT = mybir.ActivationFunctionType
AX_X = mybir.AxisListType.X

P = 128
UN = 4
BLK = 8
GB = P // BLK
PRO = 16
LN_EPS = 1e-5


def need(eng, sem, count):
    if isinstance(count, int) and count <= 0:
        return
    eng.wait_ge(sem, count)


def pipeline(eng, total, steps):
    last = max(lag for lag, _ in steps)

    def one(s, su, q):
        for lag, step in steps:
            if q is None:
                t = s - lag
                if 0 <= t < total:
                    step(t, t // UN, t % UN)
            else:
                step(q * UN + (su - lag), q + (su - lag) // UN, (su - lag) % UN)

    for s in range(PRO):
        one(s, 0, None)
    with eng.Fori(PRO // UN, total // UN) as q:
        for su in range(UN):
            one(None, su, q)
    for s in range(total, total + last):
        one(s, 0, None)


def at(tile, t):
    if isinstance(t, int):
        return tile[:, t, :]
    return tile[:, bass.ds(t, 1), :].rearrange("p a d -> p (a d)")


def graph_layers(nc, d, out):
    x, adj = d["x"], d["adj"]
    T, N, D = x.shape
    NBLK = N // BLK
    NG = T // GB
    assert N == P and D == P and T * BLK == 512

    at_scr = nc.dram_tensor("at_scr", (T, N, N), F32, kind="Internal").ap()
    an_scr = nc.dram_tensor("an_scr", (T, N, N), F32, kind="Internal").ap()

    with ExitStack() as ctx:
        def sb(name, shape):
            return ctx.enter_context(nc.sbuf_tensor(name, shape, F32))

        def sem(name):
            return ctx.enter_context(nc.semaphore(name))

        banks = [ctx.enter_context(nc.psum_tensor(f"bank{i}", [P, 512], F32)) for i in range(8)]

        ident = sb("ident", [P, P])
        below = sb("below", [P, P])
        iota = sb("iota", [P, P])
        diag16 = sb("diag16", [P, GB])
        mhalf = sb("mhalf", [P, 1])
        epsc = sb("epsc", [P, 1])
        w_nat = sb("w_nat", [P, 13, P])
        w_t = sb("w_t", [P, 13, P])
        w1 = sb("w1", [P, 2, P])
        w2 = sb("w2", [P, 2, P])
        wrel = sb("wrel", [P, P])
        wroot = sb("wroot", [P, P])
        p_bc = sb("p_bc", [P, P])
        b2_bc = sb("b2_bc", [P, P])
        brel_bc = sb("brel_bc", [P, P])
        b_nat = sb("b_nat", [16, P])
        bcol = sb("bcol", [P, 16])
        bias = sb("bias", [P, 8])
        eps1 = sb("eps1", [P, 1])
        eye_eps = sb("eye_eps", [P, P])
        junk = sb("junk", [P, 3, P])
        pn2 = sb("pn2", [P, 1])
        rpn = sb("rpn", [P, 1])

        x_res = sb("x_res", [P, T, D])
        adjn = sb("adjn", [P, T, N])
        h_nat = sb("h_nat", [P, T, D])
        h_t = sb("h_t", [P, N, T])
        coef = sb("coef", [T, NBLK, BLK, BLK])
        next_r = sb("next_r", [P, NBLK - 1, NG, BLK])

        adj_s = sb("adj_s", [P, UN, N])
        at_s = sb("at_s", [P, UN, N])
        st_a = sb("st_a", [P, UN, 6])
        mv_a = sb("mv_a", [P, UN, 2])
        rs_a = sb("rs_a", [P, UN, 2])
        xn_a = sb("xn_a", [P, UN, D])
        h_a = sb("h_a", [P, UN, D])
        score = sb("score", [P, UN, 1])
        th = sb("th", [P, UN, 1])
        dsum = sb("dsum", [P, UN, 4])
        cnt = sb("cnt", [P, UN, 4])
        pick = sb("pick", [P, 2, P])
        xa_s = sb("xa_s", [P, UN, 2 * P])
        w_s = sb("w_s", [P, 2, P])
        r_s = sb("r_s", [P, P])
        z_s = sb("z_s", [P, P])
        n_s = sb("n_s", [P, P])
        hn_s = sb("hn_s", [P, P])
        pre_s = sb("pre_s", [P, P])
        zw_s = sb("zw_s", [P, P])
        omz_s = sb("omz_s", [P, P])
        m_s = sb("m_s", [P, P])
        wn_s = sb("wn_s", [P, 2, P])
        st_b = sb("st_b", [P, UN, 6])
        mv_b = sb("mv_b", [P, UN, 2])
        rs_b = sb("rs_b", [P, UN, 2])
        xn_b = sb("xn_b", [P, 2, D])
        h_b = sb("h_b", [P, UN, D])

        s_const = sem("const_ready")
        s_wload = sem("weights_loaded")
        s_xload = [sem("x_head_loaded"), sem("x_rest_loaded")]
        s_wt_ps = sem("w_turned")
        s_wt_sb = sem("w_turned_copied")
        s_bias = sem("bias_ready")
        s_setp = sem("setup_vector_step")
        s_rpn = sem("pool_norm_ready")
        s_alone = {e: sem("lone_wait_" + e) for e in ("dve", "act", "pool", "pe")}

        adj_in = [sem(f"adj_in{i}") for i in range(UN)]
        at_out = [sem(f"at_out{i}") for i in range(UN)]
        s_anout = sem("adjn_stored")
        s_coef = sem("coef_loaded")
        at_ps, at_sb = sem("at_turned"), sem("at_copied")
        stA, mvA, rsA0, rsA = sem("stats_a"), sem("mean_var_a"), sem("var_eps_a"), sem("rstd_a")
        xnA, hA = sem("normed_a"), sem("h_a_ready")
        sc_done, th_done = sem("score_ready"), sem("tanh_score_ready")
        dv = sem("row_sum_steps")
        sb_ps = sem("score_dinv_spread")
        rk, pick_done = sem("rank_steps"), sem("pick_ready")
        adjn_done = sem("adjn_ready")
        xa_ps, xa_sb = sem("xa_product"), sem("xa_copied")
        r_ps, z_ps, n_ps = sem("r_gate_sum"), sem("z_gate_sum"), sem("n_gate_sum")
        r_done, z_done, n_done = sem("r_ready"), sem("z_ready"), sem("n_ready")
        hn_done, pre_done, zo_done, m_done, w_ready = (sem("hn_scaled"), sem("n_input_ready"), sem("zw_omz_ready"),
                                                       sem("omz_n_ready"), sem("w_ready"))
        wt_ps, wn_sb = sem("w_new_turned"), sem("w_new_copied")
        out_ps, x1_done = sem("layer0_product"), sem("x1_ready")
        stB, mvB, rsB0, rsB = sem("stats_b"), sem("mean_var_b"), sem("var_eps_b"), sem("rstd_b")
        xnB, hB, hnat = sem("normed_b"), sem("h_b_ready"), sem("h_nat_ready")
        ht_ps, ht_sb = sem("h_b_turned"), sem("h_t_ready")

        bR, bZ, bN, bAT, bSB, bXA, bW, bO = banks

        W_IH, W_HH, W_0, W_IX, W_IH1, W_CX, W_CH = 0, 3, 6, 7, 9, 11, 12

        def alone(eng, name):
            eng.sem_inc(s_alone[name], 1)

        xp_s = sb("xp_s", [P, BLK, T])
        rg = sb("rg", [P, T])
        zg = sb("zg", [P, T])
        hc = sb("hc", [P, T])
        rx = sb("rx", [P, T])
        zx = sb("zx", [P, 2, T])
        omz2 = sb("omz2", [P, 2, T])
        zxh = sb("zxh", [P, 2, T])
        t1 = sb("t1", [P, 2, T])
        p1 = sb("p1", [P, 2, T])
        p2 = sb("p2", [P, BLK, T])
        dl_s = sb("dl_s", [P, NG, BLK, GB])
        hn2 = sb("hn2", [P, NG, BLK, GB])
        cf_s = sb("cf_s", [T, BLK, BLK])
        bd_s = sb("bd_s", [P, NG, GB, BLK])
        dt_s = sb("dt_s", [P, NG, P])
        hnt_s = sb("hnt_s", [P, NG, P])

        s_xp = sem("xp_bank_full")
        s_xpr = sem("xp_ready")
        s_r2p, s_z2p, s_c2p = sem("r2_sum"), sem("z2_sum"), sem("c2_sum")
        s_r2, s_z2, s_hc, s_rx = sem("r2_ready"), sem("z2_ready"), sem("hc_ready"), sem("rx_ready")
        s_v = sem("vector_steps")
        s_hcu = sem("z2_used")
        s_cf = sem("coef_spread")
        s_cfu = sem("coef_used")
        s_cfs = sem("coef_slot_ready")
        s_dl = sem("block_changes_ready")
        s_hn = sem("block_states_ready")
        s_dtp, s_dts = sem("changes_turned"), sem("changes_copied")
        s_htp, s_hts = sem("states_turned"), sem("states_copied")
        s_bd = sem("block_diag_ready")
        s_hrow = sem("h_rows_stored")

        taken = [0]

        def slots(width=1):
            first = taken[0]
            taken[0] += UN * width
            return adjn[:, first:taken[0], :].rearrange("p (u c) n -> p u (c n)", u=UN)

        st3 = sb("st3", [P, 3, UN, 6])
        mv3 = sb("mv3", [P, 3, UN, 2])
        rs3 = sb("rs3", [P, 3, UN, 2])
        ae_in, ac_in, ae_s = slots(), slots(), slots()
        x2_s, xn2, h2_s, agg_s, hid_s = slots(), slots(), slots(), slots(), slots(2)
        x3_s, xn3, h3_s, n3_s, g3_s = slots(), slots(), slots(), slots(), slots()
        y1_s, cb_s, o_s = slots(), slots(), h_t[:, 0:2 * UN, :].rearrange("p (u c) n -> p u (c n)", u=UN)

        ae_ld = [sem(f"ae_ld{i}") for i in range(UN)]
        ac_ld = [sem(f"ac_ld{i}") for i in range(UN)]
        o_st = [sem(f"o_st{i}") for i in range(UN)]
        q_x2, q_ae = sem("x2_ready"), sem("adj_eps_ready")
        q_st = [sem(f"q_st{i}") for i in range(3)]
        q_mv = [sem(f"q_mv{i}") for i in range(3)]
        q_ve = [sem(f"q_ve{i}") for i in range(3)]
        q_rs = [sem(f"q_rs{i}") for i in range(3)]
        q_xn2, q_h2 = sem("xn2_ready"), sem("h2_ready")
        q_x2b = sem("x2b_ready")
        q_agp, q_ags = sem("agg_product"), sem("agg_copied")
        q_hip, q_his = sem("hidden_product"), sem("hidden_ready")
        q_w2p, q_x3 = sem("w2_product"), sem("x3_ready")
        q_xn3, q_h3, q_x3h, q_n3 = sem("xn3_ready"), sem("h3_ready"), sem("x3h_ready"), sem("n3_ready")
        q_n3p, q_g3 = sem("n3_turned"), sem("g3_ready")
        q_y1p, q_y1, q_cvp = sem("y1_product"), sem("y1_copied"), sem("conv_product")
        q_cb, q_o = sem("conv_biased"), sem("out_ready")

        NW = 26
        block = ctx.enter_context(nc.Block())

        @block.sync
        def _(sp):
            sp.dma_start(x_res[:, 0:PRO, :], x[0:PRO, :, :].rearrange("t n d -> n t d")).then_inc(s_xload[0], 16)
            loads = [0]

            def w(dst, src):
                sp.dma_start(dst, src).then_inc(s_wload, 16)
                loads[0] += 1

            for i, name in ((W_IH, "L0_gnn_W_ih"), (W_HH, "L0_gnn_W_hh"), (W_IX, "L1_gnn_W_ioux"),
                            (W_IH1, "L1_gnn_W_iouh"), (W_CX, "L1_gnn_W_coux"), (W_CH, "L1_gnn_W_couh")):
                c = d[name].shape[0] // P
                w(w_nat[:, i:i + c, :], d[name].rearrange("(c p) k -> p c k", p=P))
            w(w_nat[:, W_0, :], d["L0_gnn_W0"].rearrange("a p k -> (a p) k"))
            w(w1[:, :, :], d["L2_gnn_W1"].rearrange("p (c k) -> p c k", c=2))
            w(w2[:, :, :], d["L2_gnn_W2"].rearrange("(c p) k -> p c k", p=P))
            w(wrel[:, :], d["L3_gnn_W_rel"])
            w(wroot[:, :], d["L3_gnn_W_root"])
            w(p_bc[:, :], d["L0_gnn_pool_p"].partition_broadcast(P))
            w(b2_bc[:, :], d["L2_gnn_b2"].partition_broadcast(P))
            w(brel_bc[:, :], d["L3_gnn_b_rel"].partition_broadcast(P))
            w(eps1[:, :], d["L2_gnn_eps"].partition_broadcast(P))
            c0 = 0
            for name in ("L0_gnn_b_ih", "L0_gnn_b_hh", "L1_gnn_b_ioux", "L1_gnn_b_iouh", "L1_gnn_b_coux",
                         "L1_gnn_b_couh", "L2_gnn_b1", "L3_gnn_ln_gamma", "L3_gnn_ln_beta"):
                c = d[name].shape[0] // P
                w(b_nat[c0:c0 + c, :], d[name].rearrange("(c p) -> c p", p=P))
                c0 += c
            assert loads[0] == NW - 2, loads
            sp.dma_start(x_res[:, PRO:T, :], x[PRO:T, :, :].rearrange("t n d -> n t d")).then_inc(s_xload[1], 16)

            def load_adj(t, q, u):
                need(sp, at_ps, t - UN + 1)
                need(sp, adjn_done, t - UN + 1)
                src = adj[t, :, :] if isinstance(t, int) else adj[bass.ds(t, 1), :, :].rearrange("a n m -> n (a m)")
                sp.dma_start(adj_s[:, u, :], src).then_inc(adj_in[u], 16)

            def store_at(t, q, u):
                need(sp, at_sb, t + 1)
                dst = at_scr[t, :, :] if isinstance(t, int) else at_scr[bass.ds(t, 1), :, :].rearrange("a n m -> n (a m)")
                sp.dma_start(dst, at_s[:, u, :]).then_inc(at_out[u], 16)

            def store_adjn(t, q, u):
                need(sp, adjn_done, t + 1)
                dst = an_scr[t, :, :] if isinstance(t, int) else an_scr[bass.ds(t, 1), :, :].rearrange("a n m -> n (a m)")
                sp.dma_start(dst, at(adjn, t)).then_inc(s_anout, 16)

            pipeline(sp, T, [(0, load_adj), (3, store_at), (4, store_adjn)])

            sp.wait_ge(s_anout, 16 * T)
            piece = bass.AP(an_scr.tensor, 0, [[N * N, T], [BLK * N + BLK, NBLK], [N, BLK], [1, BLK]])
            for m in range(NBLK):
                sp.dma_start(coef[:, m, :, :], piece[:, m, :, :]).then_inc(s_coef, 16)
            for g in range(NG):
                for k in range(BLK):
                    src = bass.AP(an_scr.tensor, g * GB * N * N + k * N + BLK,
                                  [[N * N, GB], [BLK * N + BLK, NBLK - 1], [1, BLK]])
                    sp.dma_start(next_r[k * GB:(k + 1) * GB, :, g, :], src).then_inc(s_coef, 16)

            for m in range(NBLK):
                sp.wait_ge(s_hts, m + 1)
                for g in range(NG):
                    sp.dma_start(h_nat[m * BLK:(m + 1) * BLK, g * GB:(g + 1) * GB, :],
                                 hnt_s[:, g, :]).then_inc(s_hrow, 16)

            def load_ae(t, q, u):
                need(sp, q_ae, t - UN + 1)
                src = at_scr[t, :, :] if isinstance(t, int) else at_scr[bass.ds(t, 1), :, :].rearrange("a n m -> n (a m)")
                sp.dma_start(ae_in[:, u, :], src).then_inc(ae_ld[u], 16)

            def load_ac(t, q, u):
                need(sp, q_cvp, t - UN + 1)
                src = at_scr[t, :, :] if isinstance(t, int) else at_scr[bass.ds(t, 1), :, :].rearrange("a n m -> n (a m)")
                sp.dma_start(ac_in[:, u, :], src).then_inc(ac_ld[u], 16)

            def store_out(t, q, u):
                need(sp, q_o, t + 1)
                dst = out[t, :, :] if isinstance(t, int) else out[bass.ds(t, 1), :, :].rearrange("a n m -> n (a m)")
                sp.dma_start(dst, o_s[:, u, :]).then_inc(o_st[u], 16)

            for u in range(UN):
                sp.wait_ge(at_out[u], 16 * (T // UN))
            pipeline(sp, T, [(0, load_ae), (7, load_ac), (11, store_out)])
            for u in range(UN):
                sp.wait_ge(o_st[u], 16 * (T // UN))

        @block.gpsimd
        def _(pool):
            g = nc.gpsimd
            g.memset(mhalf[:, :], -0.5).then_inc(s_const, 1)
            g.memset(epsc[:, :], LN_EPS).then_inc(s_const, 1)
            g.memset(ident[:, :], 0.0).then_inc(s_const, 1)
            g.memset(below[:, :], 1.0).then_inc(s_const, 1)
            g.memset(diag16[:, :], 0.0).then_inc(s_const, 1)
            pool.wait_ge(s_const, 5)
            g.affine_select(out=ident[:, :], in_=ident[:, :], compare_op=ALU.not_equal, fill=1.0, base=0,
                            pattern=[[-1, P]], channel_multiplier=1).then_inc(s_const, 1)
            g.affine_select(out=below[:, :], in_=below[:, :], compare_op=ALU.is_gt, fill=0.0, base=0,
                            pattern=[[-1, P]], channel_multiplier=1).then_inc(s_const, 1)
            g.iota(iota[:, :], pattern=[[1, P]], base=0, channel_multiplier=0,
                   allow_small_or_imprecise_dtypes=True).then_inc(s_const, 1)
            for k in range(BLK):
                pool.wait_ge(s_const, 8 + k)
                g.affine_select(out=diag16[:, :], in_=diag16[:, :], compare_op=ALU.not_equal, fill=1.0,
                                base=-GB * k, pattern=[[-1, GB]], channel_multiplier=1).then_inc(s_const, 1)
            pool.wait_ge(s_setp, 1)
            g.tensor_tensor(rpn[:, :], pn2[:, :], mhalf[:, :], ALU.pow).then_inc(s_rpn, 1)

            def rstd(mv, ve_sem, mv_sem, out_sem, rs):
                def step(t, q, u):
                    need(pool, mv_sem, t + 1)
                    g.tensor_tensor(rs[:, u, 0:1], mv[:, u, 1:2], epsc[:, :], ALU.add).then_inc(ve_sem, 1)
                    need(pool, ve_sem, t + 1)
                    g.tensor_tensor(rs[:, u, 1:2], rs[:, u, 0:1], mhalf[:, :], ALU.pow).then_inc(out_sem, 1)
                return step

            def keep_h(t, q, u):
                need(pool, hB, t + 1)
                if not isinstance(t, int):
                    alone(pool, "pool")
                g.tensor_copy(at(h_nat, t), h_b[:, u, :]).then_inc(hnat, 1)

            pipeline(pool, T, [(1, rstd(mv_a, rsA0, mvA, rsA, rs_a)), (7, rstd(mv_b, rsB0, mvB, rsB, rs_b)),
                               (8, keep_h)])

            pool.wait_ge(s_coef, 16 * (NBLK + NG * BLK))
            g.tensor_copy(cf_s[:, :, :], coef[:, 0, :, :]).then_inc(s_cfs, 1)

            def block_work(m):
                need(pool, s_xp, m + 1)
                if isinstance(m, int):
                    row = next_r[:, m, :, :]
                else:
                    row = next_r[:, bass.ds(m, 1), :, :].rearrange("p a g i -> p (a g) i")
                    alone(pool, "pool")
                for gg in range(NG):
                    last = g.tensor_tensor(bd_s[:, gg, :, :], row[:, gg:gg + 1, :].to_broadcast([P, GB, BLK]),
                                           diag16[:, :].rearrange("p (b a) -> p b a", a=1).to_broadcast([P, GB, BLK]),
                                           ALU.mult)
                last.then_inc(s_bd, 1)
                need(pool, s_cf, (m + 1) * (BLK - 1))
                if isinstance(m, int):
                    src = coef[:, m + 1, :, :]
                else:
                    src = coef[:, bass.ds(m + 1, 1), :, :].rearrange("p a j i -> p (a j) i")
                    alone(pool, "pool")
                g.tensor_copy(cf_s[:, :, :], src).then_inc(s_cfs, 1)

            block_work(0)
            with pool.Fori(1, NBLK - 1) as m:
                block_work(m)

            def adj_eps(t, q, u):
                need(pool, q_agp, t - UN + 1)
                need(pool, ae_ld[u], 16 * (q + 1))
                g.tensor_tensor(ae_s[:, u, :], ae_in[:, u, :], eye_eps[:, :], ALU.add).then_inc(q_ae, 1)

            def x2b(t, q, u):
                need(pool, q_x2, t + 1)
                if not isinstance(t, int):
                    alone(pool, "pool")
                g.tensor_tensor(at(x_res, t), x2_s[:, u, :], b2_bc[:, :], ALU.add).then_inc(q_x2b, 1)

            def x3h(t, q, u):
                need(pool, q_h3, t + 1)
                if not isinstance(t, int):
                    alone(pool, "pool")
                g.tensor_tensor(at(x_res, t), x3_s[:, u, :], h3_s[:, u, :], ALU.add).then_inc(q_x3h, 1)

            def r3(i):
                return rstd(mv3[:, i, :, :], q_ve[i], q_mv[i], q_rs[i], rs3[:, i, :, :])

            pipeline(pool, T, [(1, r3(0)), (5, r3(1)), (6, r3(2)), (1, x2b), (1, adj_eps), (6, x3h)])

        @block.scalar
        def _(act):
            a = nc.scalar
            a.preload_act_table_set("sigmoid_and_others")
            for c in range(4):
                n = min(4, 13 - 4 * c)
                act.wait_ge(s_wt_ps, c + 1)
                a.activation(w_t[:, 4 * c:4 * c + n, :], banks[c][:, 0:n * P], ACT.Copy).then_inc(s_wt_sb, 1)
            a.activation(bcol[:, :], banks[3][:, P:P + 16], ACT.Copy).then_inc(s_wt_sb, 1)
            act.wait_ge(s_wt_sb, 5)
            a.activation(w_s[:, 0, :], w_t[:, W_0, :], ACT.Copy).then_inc(w_ready, 1)
            act.wait_ge(s_bias, 1)
            act.wait_ge(s_rpn, 1)

            def sig_r(t, q, u):
                need(act, r_ps, t + 1)
                need(act, hn_done, t)
                a.activation(r_s[:, :], bR[:, 0:P], ACT.Sigmoid, bias=bias[:, 0:1]).then_inc(r_done, 1)

            def sig_z(t, q, u):
                need(act, z_ps, t + 1)
                need(act, zo_done, t)
                a.activation(z_s[:, :], bZ[:, 0:P], ACT.Sigmoid, bias=bias[:, 1:2]).then_inc(z_done, 1)

            def tanh_n(t, q, u):
                need(act, pre_done, t + 1)
                need(act, m_done, t)
                a.activation(n_s[:, :], pre_s[:, :], ACT.Tanh, bias=bcol[:, 2:3]).then_inc(n_done, 1)

            def copy_at(t, q, u):
                need(act, at_out[u], 16 * q)
                need(act, xa_ps, t - UN + 1)
                need(act, at_ps, t + 1)
                a.activation(at_s[:, u, :], bAT[:, 0:P], ACT.Copy).then_inc(at_sb, 1)

            def relu_a(t, q, u):
                need(act, xa_ps, t - UN + 1)
                need(act, xnA, t + 1)
                a.activation(h_a[:, u, :], xn_a[:, u, :], ACT.Relu).then_inc(hA, 1)

            def tanh_score(t, q, u):
                need(act, pick_done, t - UN + 1)
                need(act, sc_done, t + 1)
                a.activation(th[:, u, :], score[:, u, :], ACT.Tanh, scale=rpn[:, 0:1]).then_inc(th_done, 1)

            def copy_xa(t, q, u):
                need(act, out_ps, t - UN + 1)
                need(act, xa_ps, t + 1)
                a.activation(xa_s[:, u, :], bXA[:, 0:2 * P], ACT.Copy).then_inc(xa_sb, 1)

            def copy_wn(t, q, u):
                need(act, out_ps, t - 1)
                need(act, wt_ps, t + 1)
                a.activation(wn_s[:, u % 2, :], bW[:, 0:P], ACT.Copy).then_inc(wn_sb, 1)

            def relu_b(t, q, u):
                need(act, hnat, t - UN + 1)
                need(act, ht_ps, t - UN + 1)
                need(act, xnB, t + 1)
                a.activation(h_b[:, u, :], xn_b[:, u % 2, :], ACT.Relu).then_inc(hB, 1)

            def copy_ht(t, q, u):
                need(act, wt_ps, min(t + 4, T) if isinstance(t, int) else t + 4)
                need(act, ht_ps, t + 1)
                if isinstance(t, int):
                    dst = h_t[:, :, t:t + 1]
                else:
                    alone(act, "act")
                    dst = h_t[:, :, bass.ds(t, 1)]
                a.activation(dst, bW[:, P:2 * P].rearrange("p (n a) -> p n a", a=1), ACT.Copy).then_inc(ht_sb, 1)

            pipeline(act, T, [(5, sig_r), (1, copy_at), (5, sig_z), (2, relu_a), (5, tanh_n), (3, tanh_score),
                              (4, copy_xa), (6, copy_wn), (8, relu_b), (9, copy_ht)])

            def nodes(m, last):
                for k in range(BLK):
                    n = m * BLK + k
                    need(act, s_r2p, n + 1)
                    need(act, s_rx, n)
                    a.activation(rg[:, :], bR[:, 0:T], ACT.Sigmoid, bias=bias[:, 2:3]).then_inc(s_r2, 1)
                    need(act, s_z2p, n + 1)
                    need(act, s_hcu, n)
                    a.activation(zg[:, :], bZ[:, 0:T], ACT.Sigmoid, bias=bias[:, 3:4]).then_inc(s_z2, 1)
                    need(act, s_c2p, n + 1)
                    a.activation(hc[:, :], bN[:, 0:T], ACT.Tanh, bias=bias[:, 4:5]).then_inc(s_hc, 1)
                need(act, s_hrow, 16 * NG * m)
                need(act, s_htp, m + 1)
                a.activation(hnt_s[:, :, :], bO[:, :], ACT.Copy).then_inc(s_hts, 1)

            nodes(0, False)
            with act.Fori(1, NBLK - 1) as m:
                nodes(m, False)
            nodes(NBLK - 1, True)

            def relu2(t, q, u):
                need(act, q_agp, t - UN + 1)
                need(act, q_xn2, t + 1)
                a.activation(h2_s[:, u, :], xn2[:, u, :], ACT.Relu).then_inc(q_h2, 1)

            def copy_agg(t, q, u):
                need(act, q_hip, t - UN + 1)
                need(act, q_agp, t + 1)
                a.activation(agg_s[:, u, :], banks[0][:, 0:P], ACT.Copy).then_inc(q_ags, 1)

            def hidden(t, q, u):
                need(act, q_w2p, t - UN + 1)
                need(act, q_hip, t + 1)
                for c in range(2):
                    a.activation(hid_s[:, u, c * P:(c + 1) * P], banks[1][:, c * P:(c + 1) * P], ACT.Relu,
                                 bias=bcol[:, 12 + c:13 + c]).then_inc(q_his, 1)

            def relu3(t, q, u):
                need(act, q_x3h, t - UN + 1)
                need(act, q_n3, t - UN + 1)
                need(act, q_xn3, t + 1)
                a.activation(h3_s[:, u, :], xn3[:, u, :], ACT.Relu).then_inc(q_h3, 1)

            def turn_g(t, q, u):
                need(act, q_cvp, t - UN + 1)
                need(act, q_n3p, t + 1)
                a.activation(g3_s[:, u, :], banks[3][:, 0:P], ACT.Identity, bias=bcol[:, 15:16],
                             scale=bcol[:, 14:15]).then_inc(q_g3, 1)

            def copy_y1(t, q, u):
                need(act, q_cvp, t - UN + 1)
                need(act, q_y1p, t + 1)
                a.activation(y1_s[:, u, :], banks[4][:, 0:P], ACT.Copy).then_inc(q_y1, 1)

            pipeline(act, T, [(3, copy_agg), (4, hidden), (8, turn_g), (9, copy_y1), (2, relu2), (6, relu3)])

        @block.vector
        def _(dve):
            v = nc.vector
            dve.wait_ge(s_wload, 16 * (NW - 2))
            v.scalar_tensor_tensor(out=junk[:, 0, :], in0=p_bc[:, :], scalar=1.0, in1=p_bc[:, :], op0=ALU.mult,
                                   op1=ALU.mult, accum_out=pn2[:, :]).then_inc(s_setp, 1)
            dve.wait_ge(s_wt_sb, 5)
            v.tensor_tensor(bias[:, 0:2], bcol[:, 0:2], bcol[:, 3:5], ALU.add)
            v.tensor_tensor(bias[:, 2:4], bcol[:, 6:8], bcol[:, 8:10], ALU.add)
            v.tensor_tensor(bias[:, 4:5], bcol[:, 10:11], bcol[:, 11:12], ALU.add)
            v.tensor_scalar(eps1[:, :], eps1[:, :], 1.0, None, ALU.add).then_inc(s_setp, 1)
            dve.wait_ge(s_const, 8)
            dve.wait_ge(s_setp, 2)
            v.tensor_scalar(eye_eps[:, :], ident[:, :], eps1[:, 0:1], None, ALU.mult).then_inc(s_bias, 1)

            def stats(src, st, mv, st_sem, mv_sem):
                def step(t, q, u):
                    v.bn_stats(st[:, u, :], src(t, u)).then_inc(st_sem, 1)
                    need(dve, st_sem, t + 1)
                    if not isinstance(t, int):
                        alone(dve, "dve")
                    v.bn_aggr(mv[:, u, :], st[:, u, :]).then_inc(mv_sem, 1)
                return step

            xload = [False]

            def norm_a(t, q, u):
                need(dve, hA, t - UN + 1)
                need(dve, rsA, t + 1)
                v.tensor_scalar(xn_a[:, u, :], at(x_res, t), mv_a[:, u, 0:1], rs_a[:, u, 1:2], ALU.subtract,
                                ALU.mult).then_inc(xnA, 1)
                need(dve, xnA, t + 1)
                v.scalar_tensor_tensor(out=junk[:, 0, :], in0=xn_a[:, u, :], scalar=0.0, in1=p_bc[:, :], op0=ALU.max,
                                       op1=ALU.mult, accum_out=score[:, u, :]).then_inc(sc_done, 1)

            def stats_a(t, q, u):
                if isinstance(t, int):
                    dve.wait_ge(s_xload[0 if t < PRO else 1], 16)
                elif not xload[0]:
                    dve.wait_ge(s_xload[1], 16)
                stats(lambda t, u: at(x_res, t), st_a, mv_a, stA, mvA)(t, q, u)

            def row_sum(t, q, u):
                need(dve, adj_in[u], 16 * (q + 1))
                v.tensor_reduce(dsum[:, u, 0:1], adj_s[:, u, :], AX_X, ALU.add).then_inc(dv, 1)
                need(dve, dv, t * 4 + 1)
                v.tensor_scalar(dsum[:, u, 1:2], dsum[:, u, 0:1], 0.0, dsum[:, u, 0:1], ALU.is_equal,
                                ALU.add).then_inc(dv, 1)
                need(dve, dv, t * 4 + 2)
                v.reciprocal(dsum[:, u, 2:3], dsum[:, u, 1:2]).then_inc(dv, 1)
                need(dve, dv, t * 4 + 3)
                v.tensor_scalar(dsum[:, u, 3:4], dsum[:, u, 0:1], 0.0, dsum[:, u, 2:3], ALU.not_equal,
                                ALU.mult).then_inc(dv, 1)

            def rank(t, q, u):
                need(dve, sb_ps, t + 1)
                v.tensor_scalar(junk[:, 1, :], bSB[:, 0:P], score[:, u, :], 0.0, ALU.is_gt, ALU.add,
                                accum_out=cnt[:, u, 0:1])
                v.scalar_tensor_tensor(out=junk[:, 2, :], in0=bSB[:, 0:P], scalar=score[:, u, :], in1=below[:, :],
                                       op0=ALU.is_equal, op1=ALU.mult, accum_out=cnt[:, u, 1:2]).then_inc(rk, 1)
                v.tensor_tensor(at(adjn, t), adj_s[:, u, :], bSB[:, P:2 * P], ALU.mult).then_inc(adjn_done, 1)
                need(dve, rk, t * 2 + 1)
                v.tensor_tensor(cnt[:, u, 2:3], cnt[:, u, 0:1], cnt[:, u, 1:2], ALU.add).then_inc(rk, 1)
                need(dve, xa_ps, t - 1)
                need(dve, th_done, t + 1)
                need(dve, rk, t * 2 + 2)
                v.tensor_scalar(pick[:, u % 2, :], iota[:, :], cnt[:, u, 2:3], th[:, u, :], ALU.is_equal,
                                ALU.mult).then_inc(pick_done, 1)

            def gate_n(t, q, u):
                need(dve, n_ps, t + 1)
                need(dve, r_done, t + 1)
                v.scalar_tensor_tensor(out=hn_s[:, :], in0=bN[:, P:2 * P], scalar=bcol[:, 5:6], in1=r_s[:, :],
                                       op0=ALU.add, op1=ALU.mult).then_inc(hn_done, 1)
                need(dve, hn_done, t + 1)
                v.tensor_tensor(pre_s[:, :], hn_s[:, :], bN[:, 0:P], ALU.add).then_inc(pre_done, 1)

            def gate_z(t, q, u):
                need(dve, z_done, t + 1)
                v.tensor_tensor(zw_s[:, :], z_s[:, :], w_s[:, u % 2, :], ALU.mult)
                v.tensor_scalar(omz_s[:, :], z_s[:, :], -1.0, 1.0, ALU.mult, ALU.add).then_inc(zo_done, 1)

            def new_w(t, q, u):
                need(dve, zo_done, t + 1)
                need(dve, n_done, t + 1)
                v.tensor_tensor(m_s[:, :], omz_s[:, :], n_s[:, :], ALU.mult).then_inc(m_done, 1)
                need(dve, wt_ps, t - 1)
                need(dve, m_done, t + 1)
                v.tensor_tensor(w_s[:, (u + 1) % 2, :], m_s[:, :], zw_s[:, :], ALU.add).then_inc(w_ready, 1)

            def x1(t, q, u):
                need(dve, out_ps, t + 1)
                v.tensor_tensor(at(x_res, t), at(x_res, t), bO[:, 0:P], ALU.add).then_inc(x1_done, 1)
                need(dve, x1_done, t + 1)
                if not isinstance(t, int):
                    alone(dve, "dve")
                stats(lambda t, u: at(x_res, t), st_b, mv_b, stB, mvB)(t, q, u)

            def norm_b(t, q, u):
                need(dve, hB, t - 1)
                need(dve, rsB, t + 1)
                v.tensor_scalar(xn_b[:, u % 2, :], at(x_res, t), mv_b[:, u, 0:1], rs_b[:, u, 1:2], ALU.subtract,
                                ALU.mult).then_inc(xnB, 1)

            pipeline(dve, T, [(2, norm_a), (5, gate_n), (5, gate_z), (2, row_sum), (5, new_w), (3, rank),
                              (7, x1), (1, stats_a), (8, norm_b)])

            steps = [0]

            def grouped(ap):
                return ap.rearrange("p (g b) -> p g b", g=NG)

            def nodes(m, is_last):
                VS = 80
                done = [0]

                def count(ins):
                    done[0] += 1
                    ins.then_inc(s_v, 1)
                    return done[0]

                def after(n):
                    need(dve, s_v, m * VS + n)

                need(dve, s_xp, m + 1)
                xp_bank = bAT[:, :].rearrange("p (b i) -> p i b", i=BLK)
                v.tensor_copy(xp_s[:, 0:1, :], xp_bank[:, 0:1, :]).then_inc(s_xpr, 1)
                evac = count(v.tensor_copy(xp_s[:, 1:BLK, :], xp_bank[:, 1:BLK, :]))
                for k in range(BLK):
                    n = m * BLK + k
                    h_in = h_t[:, n, :] if isinstance(m, int) else \
                        h_t[:, bass.ds(n, 1), :].rearrange("p a b -> p (a b)")
                    need(dve, s_xpr, n + 1)
                    need(dve, s_r2, n + 1)
                    v.tensor_tensor(rx[:, :], rg[:, :], xp_s[:, k, :], ALU.mult).then_inc(s_rx, 1)
                    need(dve, s_z2, n + 1)
                    c_zx = count(v.tensor_tensor(zx[:, k % 2, :], zg[:, :], xp_s[:, k, :], ALU.mult))
                    v.tensor_scalar(omz2[:, k % 2, :], zg[:, :], -1.0, 1.0, ALU.mult, ALU.add).then_inc(s_hcu, 1)
                    after(c_zx)
                    c_zxh = count(v.tensor_tensor(zxh[:, k % 2, :], zx[:, k % 2, :], h_in, ALU.subtract))
                    need(dve, s_hcu, n + 1)
                    need(dve, s_hc, n + 1)
                    c_t1 = count(v.tensor_tensor(t1[:, k % 2, :], omz2[:, k % 2, :], hc[:, :], ALU.mult))
                    if k == 0:
                        need(dve, s_dtp, m)
                        need(dve, s_htp, m)
                    after(max(c_t1, c_zxh))
                    c_dl = count(v.tensor_tensor(dl_s[:, :, k, :], grouped(t1[:, k % 2, :]), grouped(zxh[:, k % 2, :]), ALU.add))
                    if k == BLK - 1:
                        after(c_dl)
                        dve.sem_inc(s_dl, 1)
                    if k < BLK - 1:
                        rest = BLK - 1 - k
                        bank = (bSB, bXA)[k % 2]
                        need(dve, s_cf, m * (BLK - 1) + k + 1)
                        after(c_dl)
                        c_p1 = count(v.tensor_tensor(grouped(p1[:, k % 2, :]), grouped(bank[:, 0:T]), dl_s[:, :, k, :],
                                                     ALU.mult))
                        if k == 0:
                            after(evac)
                        after(c_p1)
                        v.tensor_tensor(xp_s[:, k + 1, :], xp_s[:, k + 1, :], p1[:, k % 2, :], ALU.add).then_inc(s_xpr, 1)
                        if rest > 1:
                            wide = dl_s[:, :, k, :].rearrange("p g (a b) -> p a g b", a=1)\
                                .to_broadcast([P, rest - 1, NG, GB])
                            c_p2 = count(v.tensor_tensor(
                                p2[:, 0:rest - 1, :].rearrange("p i (g b) -> p i g b", g=NG),
                                bank[:, T:rest * T].rearrange("p (i g b) -> p i g b", b=GB, g=NG), wide, ALU.mult))
                            after(c_p2)
                            c_x = count(v.tensor_tensor(xp_s[:, k + 2:BLK, :], xp_s[:, k + 2:BLK, :],
                                                        p2[:, 0:rest - 1, :], ALU.add))
                            after(c_x)
                    h = v.tensor_tensor(hn2[:, :, k, :], grouped(t1[:, k % 2, :]), grouped(zx[:, k % 2, :]), ALU.add)
                    if k < BLK - 1:
                        count(h)
                        h2 = None
                    else:
                        h.then_inc(s_hn, 1)
                    if k < BLK - 1:
                        dve.sem_inc(s_cfu, 1)
                if not is_last:
                    need(dve, s_dtp, m + 1)
                    v.tensor_copy(dt_s[:, :, :], bO[:, :]).then_inc(s_dts, 1)
                while done[0] < VS:
                    dve.sem_inc(s_v, VS - done[0])
                    done[0] = VS

            nodes(0, False)
            with dve.Fori(1, NBLK - 1) as m:
                nodes(m, False)
            nodes(NBLK - 1, True)

            dve.wait_ge(s_hrow, 16 * NG * NBLK)

            def x2(t, q, u):
                need(dve, q_x2b, t - UN + 1)
                v.tensor_tensor(x2_s[:, u, :], at(x_res, t), at(h_nat, t), ALU.add).then_inc(q_x2, 1)
                need(dve, q_x2, t + 1)
                stats(lambda t, u: x2_s[:, u, :], st3[:, 0, :, :], mv3[:, 0, :, :], q_st[0], q_mv[0])(t, q, u)

            def norm2(t, q, u):
                need(dve, q_h2, t - UN + 1)
                need(dve, q_rs[0], t + 1)
                v.tensor_scalar(xn2[:, u, :], x2_s[:, u, :], mv3[:, 0, u, 0:1], rs3[:, 0, u, 1:2], ALU.subtract,
                                ALU.mult).then_inc(q_xn2, 1)

            def x3(t, q, u):
                need(dve, q_x3h, t - UN + 1)
                need(dve, q_x2b, t + 1)
                need(dve, q_w2p, t + 1)
                v.tensor_tensor(x3_s[:, u, :], at(x_res, t), banks[2][:, 0:P], ALU.add).then_inc(q_x3, 1)
                need(dve, q_x3, t + 1)
                stats(lambda t, u: x3_s[:, u, :], st3[:, 1, :, :], mv3[:, 1, :, :], q_st[1], q_mv[1])(t, q, u)

            def norm3(t, q, u):
                need(dve, q_h3, t - UN + 1)
                need(dve, q_rs[1], t + 1)
                v.tensor_scalar(xn3[:, u, :], x3_s[:, u, :], mv3[:, 1, u, 0:1], rs3[:, 1, u, 1:2], ALU.subtract,
                                ALU.mult).then_inc(q_xn3, 1)

            def stats_h3(t, q, u):
                need(dve, q_h3, t + 1)
                stats(lambda t, u: h3_s[:, u, :], st3[:, 2, :, :], mv3[:, 2, :, :], q_st[2], q_mv[2])(t, q, u)

            def norm_h3(t, q, u):
                need(dve, q_n3p, t - UN + 1)
                need(dve, q_rs[2], t + 1)
                v.tensor_scalar(n3_s[:, u, :], h3_s[:, u, :], mv3[:, 2, u, 0:1], rs3[:, 2, u, 1:2], ALU.subtract,
                                ALU.mult).then_inc(q_n3, 1)

            def finish(t, q, u):
                need(dve, q_cvp, t + 1)
                v.tensor_tensor(cb_s[:, u, :], banks[5][:, 0:P], brel_bc[:, :], ALU.add).then_inc(q_cb, 1)
                need(dve, o_st[u], 16 * q)
                need(dve, q_x3h, t + 1)
                need(dve, q_cb, t + 1)
                v.scalar_tensor_tensor(out=o_s[:, u, :], in0=cb_s[:, u, :], scalar=0.0, in1=at(x_res, t),
                                       op0=ALU.max, op1=ALU.add).then_inc(q_o, 1)

            pipeline(dve, T, [(5, x3), (1, x2), (2, norm2), (6, norm3), (10, finish), (7, norm_h3), (6, stats_h3)])

        @block.tensor
        def _(pe):
            mm, turn = nc.tensor.matmul, nc.tensor.transpose
            pe.wait_ge(s_wload, 16 * (NW - 2))
            pe.wait_ge(s_const, 8)
            for i in range(13):
                ins = turn(banks[i // 4][:, (i % 4) * P:(i % 4 + 1) * P], w_nat[:, i, :], ident[:, :])
                if i % 4 == 3:
                    ins.then_inc(s_wt_ps, 1)
            turn(banks[3][:, P:P + 16], b_nat[:, :], ident[0:16, 0:16]).then_inc(s_wt_ps, 1)
            pe.wait_ge(s_wt_sb, 5)

            def add(out_, l, r, start=False):
                return mm(out_, l, r, start=start, stop=True, skip_group_check=True)

            def turn_adj(t, q, u):
                need(pe, at_sb, t)
                need(pe, adj_in[u], 16 * (q + 1))
                turn(bAT[:, 0:P], adj_s[:, u, :], ident[:, :]).then_inc(at_ps, 1)

            def spread(t, q, u):
                need(pe, adjn_done, t)
                need(pe, sc_done, t + 1)
                need(pe, dv, t * 4 + 4)
                turn(bSB[:, 0:P], score[:, u, :].to_broadcast([P, P]), ident[:, :])
                turn(bSB[:, P:2 * P], dsum[:, u, 3:4].to_broadcast([P, P]), ident[:, :]).then_inc(sb_ps, 1)

            def pick_rows(t, q, u):
                need(pe, xa_sb, t)
                need(pe, hA, t + 1)
                need(pe, at_sb, t + 1)
                need(pe, pick_done, t + 1)
                mm(bXA[:, 0:P], h_a[:, u, :], pick[:, u % 2, :], start=True, stop=True)
                mm(bXA[:, P:2 * P], h_a[:, u, :], at_s[:, u, :], start=True, stop=True).then_inc(xa_ps, 1)

            def gru_in(t, q, u):
                need(pe, xa_sb, t + 1)
                need(pe, r_done, t)
                need(pe, z_done, t)
                need(pe, pre_done, t)
                add(bR[:, 0:P], w_t[:, W_IH, :], xa_s[:, u, 0:P], True)
                add(bZ[:, 0:P], w_t[:, W_IH + 1, :], xa_s[:, u, 0:P], True)
                add(bN[:, 0:P], w_t[:, W_IH + 2, :], xa_s[:, u, 0:P], True)

            def gru_state(t, q, u):
                need(pe, w_ready, t + 1)
                add(bR[:, 0:P], w_t[:, W_HH, :], w_s[:, u % 2, :]).then_inc(r_ps, 1)
                add(bN[:, P:2 * P], w_t[:, W_HH + 2, :], w_s[:, u % 2, :]).then_inc(n_ps, 1)
                add(bZ[:, 0:P], w_t[:, W_HH + 1, :], w_s[:, u % 2, :]).then_inc(z_ps, 1)

            def turn_w(t, q, u):
                need(pe, wn_sb, t)
                need(pe, ht_sb, t - 3)
                need(pe, w_ready, t + 2)
                turn(bW[:, 0:P], w_s[:, (u + 1) % 2, :], ident[:, :]).then_inc(wt_ps, 1)

            def layer0(t, q, u):
                need(pe, x1_done, t)
                need(pe, wn_sb, t + 1)
                mm(bO[:, 0:P], xa_s[:, u, P:2 * P], wn_s[:, u % 2, :], start=True, stop=True).then_inc(out_ps, 1)

            def turn_h(t, q, u):
                need(pe, ht_sb, t)
                need(pe, wn_sb, min(t + 3, T) if isinstance(t, int) else t + 3)
                need(pe, hB, t + 1)
                turn(bW[:, P:2 * P], h_b[:, u, :], ident[:, :]).then_inc(ht_ps, 1)

            pipeline(pe, T, [(5, gru_state), (4, pick_rows), (7, layer0), (1, turn_adj), (3, spread), (9, turn_h),
                             (6, turn_w), (4, gru_in)])

            def gather(m, graphs):
                for b in graphs:
                    cols = adjn[:, b, m * BLK:(m + 1) * BLK] if isinstance(m, int) else \
                        adjn[:, b, bass.ds(m * BLK, BLK)]
                    ins = add(bAT[:, b * BLK:(b + 1) * BLK], h_nat[:, b, :], cols, b == 0)
                return ins

            def node_in(m, k):
                n = m * BLK + k
                return h_t[:, n, :] if isinstance(n, int) else h_t[:, bass.ds(n, 1), :].rearrange("p a b -> p (a b)")

            def gates_in(m, k):
                n = m * BLK + k
                need(pe, s_r2, n)
                need(pe, s_z2, n)
                add(bR[:, 0:T], w_t[:, W_IX, :], node_in(m, k), True)
                add(bZ[:, 0:T], w_t[:, W_IX + 1, :], node_in(m, k), True)

            def cand_in(m, k):
                need(pe, s_hc, m * BLK + k)
                add(bN[:, 0:T], w_t[:, W_CX, :], node_in(m, k), True)

            def spread_row(m, k):
                c = m * (BLK - 1) + k
                need(pe, s_cfu, c - 1)
                if k == 0:
                    need(pe, s_cfs, m + 1)
                    if not isinstance(m, int):
                        alone(pe, "pe")
                elif not isinstance(m, int):
                    alone(pe, "pe")
                bank = (bSB, bXA)[k % 2]
                for i in range(k + 1, BLK):
                    o = (i - k - 1) * T
                    ins = turn(bank[:, o:o + T], cf_s[:, k, i:i + 1].to_broadcast([T, P]), ident[0:T, 0:T])
                ins.then_inc(s_cf, 1)

            pe.wait_ge(s_anout, 16 * T)
            pe.wait_ge(hnat, T)
            pe.wait_ge(ht_sb, T)
            pe.wait_ge(x1_done, T)
            pe.wait_ge(at_sb, T)
            gather(0, range(T)).then_inc(s_xp, 1)
            gates_in(0, 0)
            spread_row(0, 0)

            def nodes(m, is_last):
                share = [0] + [9] * 6 + [10]
                share[1] = 0 if False else share[1]
                b0 = 0
                for k in range(BLK):
                    n = m * BLK + k
                    todo = list(range(b0, min(b0 + share[k], T))) if not is_last else []
                    b0 += share[k]
                    need(pe, s_xpr, n + 1)
                    add(bR[:, 0:T], w_t[:, W_IH1, :], xp_s[:, k, :]).then_inc(s_r2p, 1)
                    add(bZ[:, 0:T], w_t[:, W_IH1 + 1, :], xp_s[:, k, :]).then_inc(s_z2p, 1)
                    cand_in(m, k)
                    half = len(todo) // 3
                    if todo:
                        if k == 1:
                            need(pe, s_v, m * 80 + 1)
                            need(pe, s_hrow, 16 * NG * m)
                        gather(m + 1, todo[:half])
                    need(pe, s_rx, n + 1)
                    add(bN[:, 0:T], w_t[:, W_CH, :], rx[:, :]).then_inc(s_c2p, 1)
                    if k < BLK - 1:
                        gates_in(m, k + 1)
                        if k < BLK - 2:
                            spread_row(m, k + 1)
                    elif not is_last:
                        gates_in(m + 1, 0)
                        spread_row(m + 1, 0)
                    if todo:
                        gather(m + 1, todo[half:])
                assert is_last or b0 == T, b0
                if not is_last:
                    need(pe, s_hts, m)
                    need(pe, s_dl, m + 1)
                    for g in range(NG):
                        ins = turn(bO[:, g * P:(g + 1) * P], dl_s[:, g, :, :].rearrange("p k b -> p (k b)"), ident[:, :])
                    ins.then_inc(s_dtp, 1)
                    need(pe, s_bd, m + 1)
                    need(pe, s_dts, m + 1)
                    for g in range(NG):
                        ins = add(bAT[:, g * P:(g + 1) * P], dt_s[:, g, :],
                                  bd_s[:, g, :, :].rearrange("p b i -> p (b i)"))
                    ins.then_inc(s_xp, 1)
                need(pe, s_hn, m + 1)
                for g in range(NG):
                    ins = turn(bO[:, g * P:(g + 1) * P], hn2[:, g, :, :].rearrange("p k b -> p (k b)"), ident[:, :])
                ins.then_inc(s_htp, 1)

            nodes(0, False)
            with pe.Fori(1, NBLK - 1) as m:
                nodes(m, False)
            nodes(NBLK - 1, True)

            pe.wait_ge(s_hts, NBLK)

            def aggregate(t, q, u):
                need(pe, q_ags, t)
                need(pe, q_h2, t + 1)
                need(pe, q_ae, t + 1)
                mm(banks[0][:, 0:P], h2_s[:, u, :], ae_s[:, u, :], start=True, stop=True).then_inc(q_agp, 1)

            def mlp_in(t, q, u):
                need(pe, q_his, t * 2)
                need(pe, q_ags, t + 1)
                mm(banks[1][:, 0:P], w1[:, 0, :], agg_s[:, u, :], start=True, stop=True)
                mm(banks[1][:, P:2 * P], w1[:, 1, :], agg_s[:, u, :], start=True, stop=True).then_inc(q_hip, 1)

            def mlp_out(t, q, u):
                need(pe, q_x3, t)
                need(pe, q_his, t * 2 + 2)
                mm(banks[2][:, 0:P], hid_s[:, u, 0:P], w2[:, 0, :], start=True, stop=False)
                mm(banks[2][:, 0:P], hid_s[:, u, P:2 * P], w2[:, 1, :], start=False, stop=True).then_inc(q_w2p, 1)

            def turn_n3(t, q, u):
                need(pe, q_g3, t)
                need(pe, q_n3, t + 1)
                turn(banks[3][:, 0:P], n3_s[:, u, :], ident[:, :]).then_inc(q_n3p, 1)

            def rel(t, q, u):
                need(pe, q_y1, t)
                need(pe, q_g3, t + 1)
                mm(banks[4][:, 0:P], g3_s[:, u, :], wrel[:, :], start=True, stop=True).then_inc(q_y1p, 1)

            def conv(t, q, u):
                need(pe, q_cb, t)
                need(pe, q_y1, t + 1)
                need(pe, ac_ld[u], 16 * (q + 1))
                mm(banks[5][:, 0:P], g3_s[:, u, :], wroot[:, :], start=True, stop=False)
                mm(banks[5][:, 0:P], ac_in[:, u, :], y1_s[:, u, :], start=False, stop=True).then_inc(q_cvp, 1)

            pipeline(pe, T, [(3, aggregate), (4, mlp_in), (5, mlp_out), (8, turn_n3), (9, rel), (10, conv)])


_INS = ['x', 'adj', 'L0_gnn_pool_p', 'L0_gnn_W_ih', 'L0_gnn_W_hh', 'L0_gnn_b_ih', 'L0_gnn_b_hh', 'L0_gnn_W0',
        'L1_gnn_W_ioux', 'L1_gnn_b_ioux', 'L1_gnn_W_iouh', 'L1_gnn_b_iouh', 'L1_gnn_W_coux', 'L1_gnn_b_coux',
        'L1_gnn_W_couh', 'L1_gnn_b_couh', 'L2_gnn_eps', 'L2_gnn_W1', 'L2_gnn_b1', 'L2_gnn_W2', 'L2_gnn_b2',
        'L3_gnn_W_rel', 'L3_gnn_b_rel', 'L3_gnn_W_root', 'L3_gnn_ln_gamma', 'L3_gnn_ln_beta']


def kernel(**inputs):
    import numpy as _np
    import concourse.bacc as _bacc
    from concourse import mybir as _mybir
    from concourse.bass_utils import run_bass_kernel_spmd as _run

    nc = _bacc.Bacc("TRN2", target_bir_lowering=False, num_devices=1)
    arrays, dram = {}, {}
    for name in _INS:
        a = _np.ascontiguousarray(inputs[name])
        arrays[f"in_{name}_dram"] = a
        dram[name] = nc.dram_tensor(f"in_{name}_dram", a.shape, _mybir.dt.from_np(a.dtype), kind="ExternalInput").ap()
    out = nc.dram_tensor("out_0_dram", inputs["x"].shape, _mybir.dt.float32, kind="ExternalOutput").ap()
    graph_layers(nc, dram, out)
    r = _run(nc, [arrays], core_ids=[0])
    return r.results[0]["out_0_dram"]
```

```python
from contextlib import ExitStack

import concourse.bass as bass
from concourse import mybir

F32 = mybir.dt.float32
BF16 = mybir.dt.bfloat16
ALU = mybir.AluOpType
ACT = mybir.ActivationFunctionType
AX_X = mybir.AxisListType.X

P = 128
UN = 4
BLK = 8
GB = P // BLK
PRO = 20
LN_EPS = 1e-5


def need(eng, sem, count):
    if isinstance(count, int) and count <= 0:
        return
    eng.wait_ge(sem, count)


def pipeline(eng, total, steps):
    last = max(lag for lag, _ in steps)

    def one(s, su, q):
        for lag, step in steps:
            if q is None:
                t = s - lag
                if 0 <= t < total:
                    step(t, t // UN, t % UN)
            else:
                step(q * UN + (su - lag), q + (su - lag) // UN, (su - lag) % UN)

    for s in range(PRO):
        one(s, 0, None)
    with eng.Fori(PRO // UN, total // UN) as q:
        for su in range(UN):
            one(None, su, q)
    for s in range(total, total + last):
        one(s, 0, None)


def pairs(q, u):
    return q * 2 + u // 2 + 1


def at(tile, t):
    if isinstance(t, int):
        return tile[:, t, :]
    return tile[:, bass.ds(t, 1), :].rearrange("p a d -> p (a d)")


def rows(tensor, t):
    if isinstance(t, int):
        return tensor[t, :, :]
    return tensor[bass.ds(t, 1), :, :].rearrange("a n m -> n (a m)")


def part(tile, t, c):
    if isinstance(t, int):
        return tile[:, t, c, :]
    return tile[:, bass.ds(t, 1), c, :].rearrange("p a d -> p (a d)")


def graph_layers(nc, d, out):
    x, adj = d["x"], d["adj"]
    T, N, D = x.shape
    NBLK = N // BLK
    NG = T // GB
    assert N == P and D == P and T * BLK == 512

    at_scr = nc.dram_tensor("at_scr", (T, N, N), F32, kind="Internal").ap()
    an_scr = nc.dram_tensor("an_scr", (T, N, N), F32, kind="Internal").ap()
    x1_scr = nc.dram_tensor("x1_scr", (T, N, D), F32, kind="Internal").ap()
    h_scr = nc.dram_tensor("h_scr", (T, N, D), F32, kind="Internal").ap()

    with ExitStack() as ctx:
        def sb(name, shape):
            return ctx.enter_context(nc.sbuf_tensor(name, shape, F32))

        def sem(name):
            return ctx.enter_context(nc.semaphore(name))

        banks = [ctx.enter_context(nc.psum_tensor(f"bank{i}", [P, 512], F32)) for i in range(8)]

        ident = sb("ident", [P, P])
        below = sb("below", [P, P])
        iota = sb("iota", [P, P])
        diag16 = sb("diag16", [P, GB])
        mhalf = sb("mhalf", [P, 2])
        epsc = sb("epsc", [P, 2])
        w_nat = sb("w_nat", [P, 13, P])
        w_t = sb("w_t", [P, 13, P])
        w1 = sb("w1", [P, 2, P])
        w2 = sb("w2", [P, 2, P])
        wrr = sb("wrr", [P, 2, P])
        p_bc = sb("p_bc", [P, P])
        b2_bc = sb("b2_bc", [P, P])
        brel_bc = sb("brel_bc", [P, P])
        b_nat = sb("b_nat", [16, P])
        bcol = sb("bcol", [P, 16])
        bias = sb("bias", [P, 8])
        eps1 = sb("eps1", [P, 1])
        eye_eps = sb("eye_eps", [P, P])
        junk = sb("junk", [P, 3, P])
        junk_a = sb("junk_a", [P, P])
        pn2 = sb("pn2", [P, 1])
        rpn = sb("rpn", [P, 1])

        adjb_f = sb("adjb_f", [P, T, 3 * N // 2])
        hb_f = sb("hb_f", [P, T, 3 * D // 2])
        adjb = adjb_f[:, :, :].bitcast(BF16).rearrange("p t (c n) -> p t c n", c=3)
        hb = hb_f[:, :, :].bitcast(BF16).rearrange("p t (c n) -> p t c n", c=3)
        x_res = hb_f[:, :, 0:D]
        h_t = sb("h_t", [P, N, T])
        coef = sb("coef", [T, NBLK, BLK, BLK])
        next_r = sb("next_r", [P, NBLK - 1, NG, BLK])

        adj_s = sb("adj_s", [P, UN, N])
        slots1 = sb("slots1", [P, UN, 4, P])
        pa_s = slots1[:, :, 0:2, :]
        an_s = sb("an_s", [P, UN, N])
        ra_s, rh_s = slots1[:, :, 2, :], slots1[:, :, 3, :]
        st_a = sb("st_a", [P, UN, 6])
        mv_a = sb("mv_a", [P, UN, 2])
        rs_a = sb("rs_a", [P, UN, 3])
        h_a = sb("h_a", [P, UN, D])
        score = sb("score", [P, UN, 1])
        th = sb("th", [P, UN, 1])
        dsum = sb("dsum", [P, UN, 4])
        cnt = sb("cnt", [P, UN, 4])
        xa_s = sb("xa_s", [P, UN, 2 * P])
        w_s = sb("w_s", [P, 2, P])
        r_s = sb("r_s", [P, P])
        z_s = sb("z_s", [P, P])
        n_s = sb("n_s", [P, P])
        hn_s = sb("hn_s", [P, P])
        pre_s = sb("pre_s", [P, P])
        zw_s = sb("zw_s", [P, P])
        omz_s = sb("omz_s", [P, P])
        m_s = sb("m_s", [P, P])
        wn_s = sb("wn_s", [P, 2, P])
        st_b = sb("st_b", [P, UN, 6])
        mv_b = sb("mv_b", [P, UN, 2])
        rs_b = sb("rs_b", [P, UN, 3])
        h_b = sb("h_b", [P, UN, D])

        s_const = sem("const_ready")
        s_wload = sem("weights_loaded")
        s_xload = [sem("x_head_loaded"), sem("x_rest_loaded")]
        s_wt_ps = sem("w_turned")
        s_wt_sb = sem("w_turned_copied")
        s_bias = sem("bias_ready")
        s_setp = sem("setup_vector_step")
        s_rpn = sem("pool_norm_ready")
        s_alone = sem("lone_wait")

        adj_in = [sem(f"adj_in{i}") for i in range(UN)]
        at_out = [sem(f"at_out{i}") for i in range(UN)]
        s_anout = [sem(f"adjn_stored{i}") for i in range(UN)]
        x1_out = [sem(f"x1_stored{i}") for i in range(UN)]
        s_coef = sem("coef_loaded")
        at_ps, at_sb = sem("at_turned"), sem("at_copied")
        stA, mvA, rsA0, rsA = sem("stats_a"), sem("mean_var_a"), sem("var_eps_a"), sem("rstd_a")
        nmA, hA = sem("mean_rstd_a"), sem("h_a_ready")
        sc_done, th_done = sem("score_ready"), sem("tanh_score_ready")
        sum_done, dv = sem("row_sum_ready"), sem("row_sum_steps")
        sb_ps = sem("score_dinv_spread")
        rk, pick_done = sem("rank_steps"), sem("pick_ready")
        adjn_done = sem("adjn_ready")
        xa_ps, xa_sb = sem("xa_product"), sem("xa_copied")
        r_ps, z_ps, n_ps = sem("r_gate_sum"), sem("z_gate_sum"), sem("n_gate_sum")
        r_done, z_done, n_done = sem("r_ready"), sem("z_ready"), sem("n_ready")
        hn_done, pre_done, zo_done, m_done, w_ready, omz_done = (sem("hn_scaled"), sem("n_input_ready"), sem("zw_ready"),
                                                       sem("omz_n_ready"), sem("w_ready"), sem("omz_ready"))
        wt_ps, wn_sb = sem("w_new_turned"), sem("w_new_copied")
        out_ps, x1_done = sem("layer0_product"), sem("x1_ready")
        a1_done, ra_done, a2_done, split_done = (sem("adj_part1"), sem("adj_rest"), sem("adj_part2"),
                                                 sem("adj_part3"))
        h1_done, rh_done, h2_done = sem("h_part1"), sem("h_rest"), sem("h_part2")
        stB, mvB, rsB0, rsB = sem("stats_b"), sem("mean_var_b"), sem("var_eps_b"), sem("rstd_b")
        nmB, hB, hnat = sem("mean_rstd_b"), sem("h_b_ready"), sem("h_part3")
        ht_ps, ht_sb = sem("h_b_turned"), sem("h_t_ready")

        bR, bZ, bN, bAT, bSB, bXA, bW, bO = banks

        W_IH, W_HH, W_0, W_IX, W_IH1, W_CX, W_CH = 0, 3, 6, 7, 9, 11, 12

        def alone(eng):
            eng.sem_inc(s_alone, 1)

        xp_s = sb("xp_s", [P, BLK, T])
        rg = sb("rg", [P, T])
        zg = sb("zg", [P, T])
        hc = sb("hc", [P, T])
        rx = sb("rx", [P, T])
        zx = sb("zx", [P, 2, T])
        omz2 = sb("omz2", [P, 2, T])
        zxh = sb("zxh", [P, 2, T])
        t1 = sb("t1", [P, 2, T])
        p1 = sb("p1", [P, 2, T])
        p2 = sb("p2", [P, BLK, T])
        dl_s = sb("dl_s", [P, NG, BLK, GB])
        hn2 = sb("hn2", [P, NG, BLK, GB])
        cf_s = sb("cf_s", [T, BLK, BLK])
        bd_s = sb("bd_s", [P, NG, GB, BLK])
        dt_s = sb("dt_s", [P, NG, P])
        hnt_s = sb("hnt_s", [P, NG, P])
        hrest = sb("hrest", [P, NG, P])
        hntb = xa_s[:, :, :].rearrange("p u n -> p (u n)")[:, 0:NG * 3 * P // 2].bitcast(BF16)            .rearrange("p (g c d) -> p g c d", c=3, g=NG)
        ab_s = w_nat[:, :, :].rearrange("p i k -> p (i k)")[:, 0:T * 3 * BLK // 2].bitcast(BF16)            .rearrange("p (t c i) -> p t c i", c=3, t=T)

        s_xp = sem("xp_bank_full")
        s_xpr = sem("xp_ready")
        s_r2p, s_z2p, s_c2p = sem("r2_sum"), sem("z2_sum"), sem("c2_sum")
        s_r2, s_z2, s_hc, s_rx = sem("r2_ready"), sem("z2_ready"), sem("hc_ready"), sem("rx_ready")
        s_v = sem("vector_steps")
        s_hcu = sem("z2_used")
        s_cf = sem("coef_spread")
        s_cfu = sem("coef_used")
        s_cfs = sem("coef_slot_ready")
        s_dl = sem("block_changes_ready")
        s_hn = sem("block_states_ready")
        s_dtp, s_dts = sem("changes_turned"), sem("changes_copied")
        s_htp, s_hts = sem("states_turned"), sem("states_copied")
        s_bd = sem("block_diag_ready")
        s_hscr = sem("states_stored")
        s_h1, s_hr, s_h2, s_h3 = sem("states_part1"), sem("states_rest"), sem("states_part2"), sem("states_part3")
        s_hrow = sem("part_rows_stored")
        s_ab = sem("next_adjacency_ready")

        taken = [0]
        slot_space = adjb_f[:, :, :].rearrange("p t c -> p (t c)")

        def slots(width=1):
            first = taken[0]
            taken[0] += UN * width
            return slot_space[:, first * P:taken[0] * P].rearrange("p (u n) -> p u n", u=UN)

        st3 = sb("st3", [P, 3, UN, 6])
        mv3 = sb("mv3", [P, 3, UN, 2])
        rs3 = sb("rs3", [P, 3, UN, 3])
        ae_in, ac_in, ae_s = slots(), slots(), slots()
        x2_s, h2_s, agg_s, hid_s = slots(), slots(), slots(), slots(2)
        hid_s = hid_s.rearrange("p (a c) n -> p a c n", c=2)
        x3_s, h3_s, n3_s, g3_s = slots(), slots(), slots(), slots()
        h_in = slots()
        y1_s, cb_s, o_s = slots(), slots(), h_t[:, 0:2 * UN, :].rearrange("p (u c) n -> p u (c n)", u=UN)

        in_ld = [sem(f"graph_in{i}") for i in range(UN)]
        ac_ld = [sem(f"ac_ld{i}") for i in range(UN)]
        o_st = [sem(f"o_st{i}") for i in range(UN)]
        q_x2, q_ae = sem("x2_ready"), sem("adj_eps_ready")
        q_st = [sem(f"q_st{i}") for i in range(3)]
        q_mv = [sem(f"q_mv{i}") for i in range(3)]
        q_ve = [sem(f"q_ve{i}") for i in range(3)]
        q_rs = [sem(f"q_rs{i}") for i in range(3)]
        q_nm = [sem(f"q_nm{i}") for i in range(3)]
        q_h2 = sem("h2_ready")
        q_x2b = sem("x2b_ready")
        q_agp, q_ags = sem("agg_product"), sem("agg_copied")
        q_hip, q_his = sem("hidden_product"), sem("hidden_ready")
        q_w2p, q_x3 = sem("w2_product"), sem("x3_ready")
        q_h3, q_x3h, q_n3 = sem("h3_ready"), sem("x3h_ready"), sem("n3_ready")
        q_n3p, q_g3 = sem("n3_turned"), sem("g3_ready")
        q_y1p, q_y1, q_cvp = sem("y1_product"), sem("y1_copied"), sem("conv_product")
        q_cb, q_o = sem("conv_biased"), sem("out_ready")

        NW = 26
        block = ctx.enter_context(nc.Block())

        @block.sync
        def _(sp):
            sp.dma_start(x_res[:, 0:PRO, :], x[0:PRO, :, :].rearrange("t n d -> n t d")).then_inc(s_xload[0], 16)
            loads = [0]

            def w(dst, src):
                sp.dma_start(dst, src).then_inc(s_wload, 16)
                loads[0] += 1

            for i, name in ((W_IH, "L0_gnn_W_ih"), (W_HH, "L0_gnn_W_hh"), (W_IX, "L1_gnn_W_ioux"),
                            (W_IH1, "L1_gnn_W_iouh"), (W_CX, "L1_gnn_W_coux"), (W_CH, "L1_gnn_W_couh")):
                c = d[name].shape[0] // P
                w(w_nat[:, i:i + c, :], d[name].rearrange("(c p) k -> p c k", p=P))
            w(w_nat[:, W_0, :], d["L0_gnn_W0"].rearrange("a p k -> (a p) k"))
            w(w1[:, :, :], d["L2_gnn_W1"].rearrange("p (c k) -> p c k", c=2))
            w(w2[:, :, :], d["L2_gnn_W2"].rearrange("(c p) k -> p c k", p=P))
            w(wrr[:, 0, :], d["L3_gnn_W_rel"])
            w(wrr[:, 1, :], d["L3_gnn_W_root"])
            w(p_bc[:, :], d["L0_gnn_pool_p"].partition_broadcast(P))
            w(b2_bc[:, :], d["L2_gnn_b2"].partition_broadcast(P))
            w(brel_bc[:, :], d["L3_gnn_b_rel"].partition_broadcast(P))
            w(eps1[:, :], d["L2_gnn_eps"].partition_broadcast(P))
            c0 = 0
            for name in ("L0_gnn_b_ih", "L0_gnn_b_hh", "L1_gnn_b_ioux", "L1_gnn_b_iouh", "L1_gnn_b_coux",
                         "L1_gnn_b_couh", "L2_gnn_b1", "L3_gnn_ln_gamma", "L3_gnn_ln_beta"):
                c = d[name].shape[0] // P
                w(b_nat[c0:c0 + c, :], d[name].rearrange("(c p) -> c p", p=P))
                c0 += c
            assert loads[0] == NW - 2, loads
            sp.dma_start(x_res[:, PRO:T, :], x[PRO:T, :, :].rearrange("t n d -> n t d")).then_inc(s_xload[1], 16)

            def load_adj(t, q, u):
                need(sp, at_ps, t - UN + 1)
                need(sp, sum_done, t - UN + 1)
                need(sp, adjn_done, t - UN + 1)
                src = rows(adj, t)
                sp.dma_start(adj_s[:, u, :], src).then_inc(adj_in[u], 16)

            def store_at(t, q, u):
                need(sp, at_sb, t + 1)
                dst = rows(at_scr, t)
                sp.dma_start(dst, pa_s[:, u, 1, :]).then_inc(at_out[u], 16)

            def store_adjn(t, q, u):
                need(sp, adjn_done, t + 1)
                dst = rows(an_scr, t)
                sp.dma_start(dst, an_s[:, u, :]).then_inc(s_anout[u], 16)

            def store_x1(t, q, u):
                need(sp, h1_done, t - UN + 1)
                if not isinstance(t, int):
                    alone(sp)
                need(sp, x1_done, t + 1)
                sp.dma_start(rows(x1_scr, t), at(x_res, t)).then_inc(x1_out[u], 16)

            pipeline(sp, T, [(0, load_adj), (3, store_at), (5, store_adjn), (10, store_x1)])

            for u in range(UN):
                sp.wait_ge(s_anout[u], 16 * (T // UN))
            piece = bass.AP(an_scr.tensor, 0, [[N * N, T], [BLK * N + BLK, NBLK], [N, BLK], [1, BLK]])
            for m in range(NBLK):
                sp.dma_start(coef[:, m, :, :], piece[:, m, :, :]).then_inc(s_coef, 16)
            for g in range(NG):
                for k in range(BLK):
                    src = bass.AP(an_scr.tensor, g * GB * N * N + k * N + BLK,
                                  [[N * N, GB], [BLK * N + BLK, NBLK - 1], [1, BLK]])
                    sp.dma_start(next_r[k * GB:(k + 1) * GB, :, g, :], src).then_inc(s_coef, 16)

            for m in range(NBLK):
                sp.wait_ge(s_hts, m + 1)
                for g in range(NG):
                    dst = bass.AP(h_scr.tensor, g * GB * N * D + m * BLK * D, [[D, BLK], [N * D, GB], [1, D]])
                    sp.dma_start(dst, hnt_s[:, g, :]).then_inc(s_hscr, 16)
                if m < NBLK - 1:
                    sp.wait_ge(s_h3, m + 1)
                    for g in range(NG):
                        sp.dma_start(hb[m * BLK:(m + 1) * BLK, g * GB:(g + 1) * GB, :, :],
                                     hntb[:, g, :, :]).then_inc(s_hrow, 16)

            def load_ae(t, q, u):
                need(sp, q_ae, t - UN + 1)
                src = rows(at_scr, t)
                sp.dma_start(ae_in[:, u, :], src).then_inc(in_ld[u], 16)

            def load_x(t, q, u):
                need(sp, q_x2, t - UN + 1)
                sp.dma_start(h_in[:, u, :], rows(h_scr, t)).then_inc(in_ld[u], 16)
                sp.dma_start(at(x_res, t), rows(x1_scr, t)).then_inc(in_ld[u], 16)

            def load_ac(t, q, u):
                need(sp, q_cvp, t - UN + 1)
                src = rows(at_scr, t)
                sp.dma_start(ac_in[:, u, :], src).then_inc(ac_ld[u], 16)

            def store_out(t, q, u):
                need(sp, q_o, t + 1)
                dst = rows(out, t)
                sp.dma_start(dst, o_s[:, u, :]).then_inc(o_st[u], 16)

            for u in range(UN):
                sp.wait_ge(at_out[u], 16 * (T // UN))
                sp.wait_ge(x1_out[u], 16 * (T // UN))
            sp.wait_ge(s_hscr, 16 * NG * NBLK)
            sp.wait_ge(s_hrow, 16 * NG * (NBLK - 1))
            sp.wait_ge(s_xp, NBLK)
            pipeline(sp, T, [(0, load_x), (0, load_ae), (11, load_ac), (16, store_out)])
            for u in range(UN):
                sp.wait_ge(o_st[u], 16 * (T // UN))

        @block.gpsimd
        def _(pool):
            g = nc.gpsimd
            g.memset(mhalf[:, :], -0.5).then_inc(s_const, 1)
            g.memset(epsc[:, :], LN_EPS).then_inc(s_const, 1)
            g.memset(ident[:, :], 0.0).then_inc(s_const, 1)
            g.memset(below[:, :], 1.0).then_inc(s_const, 1)
            g.memset(diag16[:, :], 0.0).then_inc(s_const, 1)
            pool.wait_ge(s_const, 5)
            g.affine_select(out=ident[:, :], in_=ident[:, :], compare_op=ALU.not_equal, fill=1.0, base=0,
                            pattern=[[-1, P]], channel_multiplier=1).then_inc(s_const, 1)
            g.affine_select(out=below[:, :], in_=below[:, :], compare_op=ALU.is_gt, fill=0.0, base=0,
                            pattern=[[-1, P]], channel_multiplier=1).then_inc(s_const, 1)
            g.iota(iota[:, :], pattern=[[1, P]], base=0, channel_multiplier=0,
                   allow_small_or_imprecise_dtypes=True).then_inc(s_const, 1)
            for k in range(BLK):
                pool.wait_ge(s_const, 8 + k)
                g.affine_select(out=diag16[:, :], in_=diag16[:, :], compare_op=ALU.not_equal, fill=1.0,
                                base=-GB * k, pattern=[[-1, GB]], channel_multiplier=1).then_inc(s_const, 1)
            pool.wait_ge(s_setp, 1)
            g.tensor_tensor(rpn[:, :], pn2[:, :], mhalf[:, 0:1], ALU.pow).then_inc(s_rpn, 1)

            def rstd(mv, ve_sem, mv_sem, out_sem, rs):
                def step(t, q, u):
                    if u % 2 == 0:
                        return
                    two = slice(u - 1, u + 1)
                    need(pool, mv_sem, t + 1)
                    g.tensor_tensor(rs[:, two, 0:1], mv[:, two, 1:2], epsc[:, 0:2].rearrange("p (a b) -> p a b", b=1),
                                    ALU.add).then_inc(ve_sem, 1)
                    need(pool, ve_sem, pairs(q, u))
                    g.tensor_tensor(rs[:, two, 1:2], rs[:, two, 0:1], mhalf[:, 0:2].rearrange("p (a b) -> p a b", b=1),
                                    ALU.pow).then_inc(out_sem, 1)
                return step

            def rest(done, whole, left, parts, i, out_sem):
                def step(t, q, u):
                    need(pool, done, t + 1)
                    if not isinstance(t, int):
                        alone(pool)
                    dst = left[:, u, :] if i == 0 else part(parts, t, 2)
                    g.tensor_tensor(dst, whole[:, u, :], part(parts, t, i), ALU.subtract).then_inc(out_sem, 1)
                return step

            pipeline(pool, T, [(6, rest(a1_done, an_s, ra_s, adjb, 0, ra_done)),
                               (8, rest(a2_done, ra_s, None, adjb, 1, split_done)),
                               (1, rstd(mv_a, rsA0, mvA, rsA, rs_a)), (9, rstd(mv_b, rsB0, mvB, rsB, rs_b)),
                               (12, rest(h1_done, h_b, rh_s, hb, 0, rh_done)),
                               (13, rest(h2_done, rh_s, None, hb, 1, hnat))])

            pool.wait_ge(s_coef, 16 * (NBLK + NG * BLK))
            g.tensor_copy(cf_s[:, :, :], coef[:, 0, :, :]).then_inc(s_cfs, 1)

            def block_work(m):
                need(pool, s_xp, m + 1)
                if isinstance(m, int):
                    row = next_r[:, m, :, :]
                else:
                    row = next_r[:, bass.ds(m, 1), :, :].rearrange("p a g i -> p (a g) i")
                    alone(pool)
                for gg in range(NG):
                    last = g.tensor_tensor(bd_s[:, gg, :, :], row[:, gg:gg + 1, :].to_broadcast([P, GB, BLK]),
                                           diag16[:, :].rearrange("p (b a) -> p b a", a=1).to_broadcast([P, GB, BLK]),
                                           ALU.mult)
                last.then_inc(s_bd, 1)
                need(pool, s_cf, (m + 1) * (BLK - 1))
                if isinstance(m, int):
                    src = coef[:, m + 1, :, :]
                else:
                    src = coef[:, bass.ds(m + 1, 1), :, :].rearrange("p a j i -> p (a j) i")
                    alone(pool)
                g.tensor_copy(cf_s[:, :, :], src).then_inc(s_cfs, 1)

            def split_states(m):
                need(pool, s_h1, m + 1)
                g.tensor_tensor(hrest[:, :, :], hnt_s[:, :, :], hntb[:, :, 0, :], ALU.subtract).then_inc(s_hr, 1)
                need(pool, s_h2, m + 1)
                g.tensor_tensor(hntb[:, :, 2, :], hrest[:, :, :], hntb[:, :, 1, :], ALU.subtract).then_inc(s_h3, 1)

            block_work(0)
            with pool.Fori(1, NBLK - 1) as m:
                split_states(m - 1)
                block_work(m)
            split_states(NBLK - 2)

            def adj_eps(t, q, u):
                need(pool, q_agp, t - UN + 1)
                need(pool, in_ld[u], 48 * (q + 1))
                g.tensor_tensor(ae_s[:, u, :], ae_in[:, u, :], eye_eps[:, :], ALU.add).then_inc(q_ae, 1)

            def x2b(t, q, u):
                need(pool, q_x2, t + 1)
                if not isinstance(t, int):
                    alone(pool)
                g.tensor_tensor(at(x_res, t), x2_s[:, u, :], b2_bc[:, :], ALU.add).then_inc(q_x2b, 1)

            def x3h(t, q, u):
                need(pool, q_h3, t + 1)
                if not isinstance(t, int):
                    alone(pool)
                g.tensor_tensor(at(x_res, t), x3_s[:, u, :], h3_s[:, u, :], ALU.add).then_inc(q_x3h, 1)

            def r3(i):
                return rstd(mv3[:, i, :, :], q_ve[i], q_mv[i], q_rs[i], rs3[:, i, :, :])

            pipeline(pool, T, [(1, adj_eps), (9, x3h), (1, r3(0)), (7, r3(1)), (10, r3(2)), (1, x2b)])

        @block.scalar
        def _(act):
            a = nc.scalar
            a.preload_act_table_set("sigmoid_and_others")
            for c in range(4):
                n = min(4, 13 - 4 * c)
                act.wait_ge(s_wt_ps, c + 1)
                a.activation(w_t[:, 4 * c:4 * c + n, :], banks[c][:, 0:n * P], ACT.Copy).then_inc(s_wt_sb, 1)
            a.activation(bcol[:, :], banks[3][:, P:P + 16], ACT.Copy).then_inc(s_wt_sb, 1)
            act.wait_ge(s_wt_sb, 5)
            a.activation(w_s[:, 0, :], w_t[:, W_0, :], ACT.Copy).then_inc(w_ready, 1)
            act.wait_ge(s_bias, 1)
            act.wait_ge(s_rpn, 1)

            def sig_r(t, q, u):
                need(act, r_ps, t + 1)
                need(act, hn_done, t)
                a.activation(r_s[:, :], bR[:, (u % 2) * P:(u % 2 + 1) * P], ACT.Sigmoid, bias=bias[:, 0:1]).then_inc(r_done, 1)

            def sig_z(t, q, u):
                need(act, z_ps, t + 1)
                need(act, w_ready, t + 1)
                a.activation(z_s[:, :], bZ[:, (u % 2) * P:(u % 2 + 1) * P], ACT.Sigmoid,
                             bias=bias[:, 1:2]).then_inc(z_done, 1)

            def tanh_n(t, q, u):
                need(act, pre_done, t + 1)
                need(act, m_done, t)
                a.activation(n_s[:, :], pre_s[:, :], ACT.Tanh, bias=bcol[:, 2:3]).then_inc(n_done, 1)

            def copy_at(t, q, u):
                need(act, at_out[u], 16 * q)
                need(act, xa_ps, t - UN + 1)
                need(act, at_ps, t + 1)
                a.activation(pa_s[:, u, 1, :], bAT[:, 0:P], ACT.Copy).then_inc(at_sb, 1)

            def row_sum(t, q, u):
                need(act, dv, (t - UN + 1) * 3)
                need(act, sum_done, t)
                need(act, adj_in[u], 16 * (q + 1))
                a.activation(junk_a[:, :], adj_s[:, u, :], ACT.Copy, accum_out=dsum[:, u, 0:1]).then_inc(sum_done, 1)

            def relu_a(t, q, u):
                need(act, xa_ps, t - UN + 1)
                need(act, nmA, q * 2 + u // 2 + 1)
                a.activation(h_a[:, u, :], at(x_res, t), ACT.Relu, bias=rs_a[:, u, 2:3],
                             scale=rs_a[:, u, 1:2]).then_inc(hA, 1)

            def tanh_score(t, q, u):
                need(act, pick_done, t - UN + 1)
                need(act, sc_done, t + 1)
                a.activation(th[:, u, :], score[:, u, :], ACT.Tanh, scale=rpn[:, 0:1]).then_inc(th_done, 1)

            def copy_xa(t, q, u):
                need(act, out_ps, t - UN + 1)
                need(act, xa_ps, t + 1)
                a.activation(xa_s[:, u, :], bXA[:, 0:2 * P], ACT.Copy).then_inc(xa_sb, 1)

            def copy_wn(t, q, u):
                need(act, out_ps, t - 1)
                need(act, wt_ps, t + 1)
                a.activation(wn_s[:, u % 2, :], bW[:, 0:P], ACT.Copy).then_inc(wn_sb, 1)

            def relu_b(t, q, u):
                need(act, rh_done, t - UN + 1)
                need(act, ht_ps, t - UN + 1)
                need(act, nmB, q * 2 + u // 2 + 1)
                a.activation(h_b[:, u, :], at(x_res, t), ACT.Relu, bias=rs_b[:, u, 2:3],
                             scale=rs_b[:, u, 1:2]).then_inc(hB, 1)

            def split_h1(t, q, u):
                need(act, x1_out[u], 16 * (q + 1))
                need(act, hB, t + 1)
                if not isinstance(t, int):
                    alone(act)
                a.activation(part(hb, t, 0), h_b[:, u, :], ACT.Copy).then_inc(h1_done, 1)

            def split_a1(t, q, u):
                need(act, adjn_done, t + 1)
                if not isinstance(t, int):
                    alone(act)
                a.activation(part(adjb, t, 0), an_s[:, u, :], ACT.Copy).then_inc(a1_done, 1)

            def split_a2(t, q, u):
                need(act, ra_done, t + 1)
                if not isinstance(t, int):
                    alone(act)
                a.activation(part(adjb, t, 1), ra_s[:, u, :], ACT.Copy).then_inc(a2_done, 1)

            def split_h2(t, q, u):
                need(act, rh_done, t + 1)
                if not isinstance(t, int):
                    alone(act)
                a.activation(part(hb, t, 1), rh_s[:, u, :], ACT.Copy).then_inc(h2_done, 1)

            def copy_ht(t, q, u):
                need(act, wt_ps, min(t + 4, T) if isinstance(t, int) else t + 4)
                need(act, ht_ps, t + 1)
                if isinstance(t, int):
                    dst = h_t[:, :, t:t + 1]
                else:
                    alone(act)
                    dst = h_t[:, :, bass.ds(t, 1)]
                a.activation(dst, bW[:, P:2 * P].rearrange("p (n a) -> p n a", a=1), ACT.Copy).then_inc(ht_sb, 1)

            pipeline(act, T, [(7, sig_r), (4, tanh_score), (7, sig_z), (2, row_sum), (7, tanh_n), (2, copy_at),
                              (5, copy_xa), (3, relu_a), (11, relu_b), (8, copy_wn), (5, split_a1), (7, split_a2),
                              (12, split_h1), (11, copy_ht), (13, split_h2)])

            adjb_rows = adjb.rearrange("p t c n -> p (t c) n")

            def next_adj(m, piece):
                first = slice(piece * GB * 3, (piece + 1) * GB * 3)
                if isinstance(m, int):
                    src = adjb_rows[:, first, m * BLK:(m + 1) * BLK]
                else:
                    src = adjb_rows[:, first, bass.ds(m * BLK, BLK)]
                a.activation(ab_s[:, piece * GB:(piece + 1) * GB, :, :].rearrange("p t c i -> p (t c) i"), src,
                             ACT.Copy).then_inc(s_ab, 1)

            act.wait_ge(split_done, T)
            for piece in range(NG):
                next_adj(0, piece)

            def nodes(m, is_last):
                for k in range(BLK):
                    n = m * BLK + k
                    col = slice(k * T, (k + 1) * T)
                    need(act, s_r2p, n + 1)
                    need(act, s_rx, n)
                    a.activation(rg[:, :], bR[:, col], ACT.Sigmoid, bias=bias[:, 2:3]).then_inc(s_r2, 1)
                    need(act, s_z2p, n + 1)
                    need(act, s_hcu, n)
                    a.activation(zg[:, :], bZ[:, col], ACT.Sigmoid, bias=bias[:, 3:4]).then_inc(s_z2, 1)
                    need(act, s_c2p, n + 1)
                    a.activation(hc[:, :], bN[:, col], ACT.Tanh, bias=bias[:, 4:5]).then_inc(s_hc, 1)
                    if k < NG and not is_last:
                        next_adj(m + 1, k)
                    if k == 0 and not (isinstance(m, int) and m == 0):
                        need(act, s_hr, m)
                        a.activation(hntb[:, :, 1, :], hrest[:, :, :], ACT.Copy).then_inc(s_h2, 1)
                need(act, s_hscr, 16 * NG * m)
                need(act, s_htp, m + 1)
                a.activation(hnt_s[:, :, :], bW[:, :], ACT.Copy).then_inc(s_hts, 1)
                if not is_last:
                    need(act, s_hrow, 16 * NG * m)
                    need(act, s_hts, m + 1)
                    a.activation(hntb[:, :, 0, :], hnt_s[:, :, :], ACT.Copy).then_inc(s_h1, 1)

            nodes(0, False)
            with act.Fori(1, NBLK - 1) as m:
                nodes(m, False)
            nodes(NBLK - 1, True)

            def relu2(t, q, u):
                need(act, q_agp, t - UN + 1)
                need(act, q_nm[0], q * 2 + u // 2 + 1)
                a.activation(h2_s[:, u, :], x2_s[:, u, :], ACT.Relu, bias=rs3[:, 0, u, 2:3],
                             scale=rs3[:, 0, u, 1:2]).then_inc(q_h2, 1)

            def copy_agg(t, q, u):
                need(act, q_hip, (t - UN + 1) // 2 if isinstance(t, int) else 2 * q + (u // 2) - 1)
                need(act, q_agp, t + 1)
                a.activation(agg_s[:, u, :], (banks[0], banks[7])[u % 2][:, 0:P], ACT.Copy).then_inc(q_ags, 1)

            def hidden(t, q, u):
                if u % 2 == 0:
                    return
                need(act, q_w2p, t - UN + 1)
                need(act, q_hip, q * 2 + u // 2 + 1)
                for c in range(2):
                    a.activation(hid_s[:, u // 2, c, :], banks[1][:, 2 * c * P:2 * (c + 1) * P], ACT.Relu,
                                 bias=bcol[:, 12 + c:13 + c]).then_inc(q_his, 1)

            def relu3(t, q, u):
                need(act, q_x3h, t - UN + 1)
                need(act, q_n3, t - UN + 1)
                need(act, q_nm[1], q * 2 + u // 2 + 1)
                a.activation(h3_s[:, u, :], x3_s[:, u, :], ACT.Relu, bias=rs3[:, 1, u, 2:3],
                             scale=rs3[:, 1, u, 1:2]).then_inc(q_h3, 1)

            def norm_h3(t, q, u):
                need(act, q_n3p, t - UN + 1)
                need(act, q_nm[2], q * 2 + u // 2 + 1)
                a.activation(n3_s[:, u, :], h3_s[:, u, :], ACT.Identity, bias=rs3[:, 2, u, 2:3],
                             scale=rs3[:, 2, u, 1:2]).then_inc(q_n3, 1)

            def turn_g(t, q, u):
                need(act, q_cvp, t - UN + 1)
                need(act, q_n3p, t + 1)
                a.activation(g3_s[:, u, :], banks[3][:, 0:P], ACT.Identity, bias=bcol[:, 15:16],
                             scale=bcol[:, 14:15]).then_inc(q_g3, 1)

            def copy_y1(t, q, u):
                need(act, q_cvp, t - UN + 1)
                need(act, q_y1p, t + 1)
                a.activation(y1_s[:, u, :], banks[4 + u % 2][:, 0:P], ACT.Copy).then_inc(q_y1, 1)

            pipeline(act, T, [(4, copy_agg), (14, copy_y1), (13, turn_g), (3, relu2), (9, relu3), (12, norm_h3),
                              (5, hidden)])

        @block.vector
        def _(dve):
            v = nc.vector
            dve.wait_ge(s_wload, 16 * (NW - 2))
            v.scalar_tensor_tensor(out=junk[:, 0, :], in0=p_bc[:, :], scalar=1.0, in1=p_bc[:, :], op0=ALU.mult,
                                   op1=ALU.mult, accum_out=pn2[:, :]).then_inc(s_setp, 1)
            dve.wait_ge(s_wt_sb, 5)
            v.tensor_tensor(bias[:, 0:2], bcol[:, 0:2], bcol[:, 3:5], ALU.add)
            v.tensor_tensor(bias[:, 2:4], bcol[:, 6:8], bcol[:, 8:10], ALU.add)
            v.tensor_tensor(bias[:, 4:5], bcol[:, 10:11], bcol[:, 11:12], ALU.add)
            v.tensor_scalar(eps1[:, :], eps1[:, :], 1.0, None, ALU.add).then_inc(s_setp, 1)
            dve.wait_ge(s_const, 8)
            dve.wait_ge(s_setp, 2)
            v.tensor_scalar(eye_eps[:, :], ident[:, :], eps1[:, 0:1], None, ALU.mult).then_inc(s_bias, 1)

            def spread_of(src, st, st_sem):
                def step(t, q, u):
                    v.bn_stats(st[:, u, :], src(t, u)).then_inc(st_sem, 1)
                return step

            def aggregate(st, mv, st_sem, mv_sem):
                def step(t, q, u):
                    need(dve, st_sem, t + 1)
                    if not isinstance(t, int):
                        alone(dve)
                    v.bn_aggr(mv[:, u, :], st[:, u, :]).then_inc(mv_sem, 1)
                return step

            xload = [False]

            def mean_rstd(mv, rs, rs_sem, h_sem, out_sem):
                def step(t, q, u):
                    if u % 2 == 0:
                        return
                    two = slice(u - 1, u + 1)
                    need(dve, h_sem, t - UN + 1)
                    need(dve, rs_sem, pairs(q, u))
                    v.scalar_tensor_tensor(out=rs[:, two, 2:3], in0=mv[:, two, 0:1], scalar=-1.0, in1=rs[:, two, 1:2],
                                           op0=ALU.mult, op1=ALU.mult).then_inc(out_sem, 1)
                return step

            def score_a(t, q, u):
                need(dve, hA, t + 1)
                v.scalar_tensor_tensor(out=junk[:, 0, :], in0=h_a[:, u, :], scalar=1.0, in1=p_bc[:, :], op0=ALU.mult,
                                       op1=ALU.mult, accum_out=score[:, u, :]).then_inc(sc_done, 1)

            def stats_a(t, q, u):
                if isinstance(t, int):
                    dve.wait_ge(s_xload[0 if t < PRO else 1], 16)
                elif not xload[0]:
                    dve.wait_ge(s_xload[1], 16)
                spread_of(lambda t, u: at(x_res, t), st_a, stA)(t, q, u)

            def sum2(t, q, u):
                need(dve, sum_done, t + 1)
                v.tensor_scalar(dsum[:, u, 1:2], dsum[:, u, 0:1], 0.0, dsum[:, u, 0:1], ALU.is_equal,
                                ALU.add).then_inc(dv, 1)

            def sum3(t, q, u):
                need(dve, dv, t * 3 + 1)
                v.reciprocal(dsum[:, u, 2:3], dsum[:, u, 1:2]).then_inc(dv, 1)

            def sum4(t, q, u):
                need(dve, dv, t * 3 + 2)
                v.tensor_scalar(dsum[:, u, 3:4], dsum[:, u, 0:1], 0.0, dsum[:, u, 2:3], ALU.not_equal,
                                ALU.mult).then_inc(dv, 1)

            def rank1(t, q, u):
                need(dve, sb_ps, t + 1)
                v.tensor_scalar(junk[:, 1, :], bSB[:, 0:P], score[:, u, :], 0.0, ALU.is_gt, ALU.add,
                                accum_out=cnt[:, u, 0:1])
                v.scalar_tensor_tensor(out=junk[:, 2, :], in0=bSB[:, 0:P], scalar=score[:, u, :], in1=below[:, :],
                                       op0=ALU.is_equal, op1=ALU.mult, accum_out=cnt[:, u, 1:2]).then_inc(rk, 1)

            def scale_adj(t, q, u):
                need(dve, s_anout[u], 16 * q)
                need(dve, split_done, t - UN + 1)
                v.tensor_tensor(an_s[:, u, :], adj_s[:, u, :], bSB[:, P:2 * P], ALU.mult).then_inc(adjn_done, 1)

            def rank2(t, q, u):
                need(dve, rk, t * 2 + 1)
                v.tensor_tensor(cnt[:, u, 2:3], cnt[:, u, 0:1], cnt[:, u, 1:2], ALU.add).then_inc(rk, 1)

            def rank3(t, q, u):
                need(dve, xa_ps, t - UN + 1)
                need(dve, th_done, t + 1)
                need(dve, rk, t * 2 + 2)
                v.tensor_scalar(pa_s[:, u, 0, :], iota[:, :], cnt[:, u, 2:3], th[:, u, :], ALU.is_equal,
                                ALU.mult).then_inc(pick_done, 1)

            def gate_n(t, q, u):
                need(dve, n_ps, t + 1)
                need(dve, r_done, t + 1)
                v.scalar_tensor_tensor(out=hn_s[:, :], in0=bN[:, 2 * P + (u % 2) * P:3 * P + (u % 2) * P],
                                       scalar=bcol[:, 5:6], in1=r_s[:, :],
                                       op0=ALU.add, op1=ALU.mult).then_inc(hn_done, 1)

            def gate_n2(t, q, u):
                need(dve, hn_done, t + 1)
                v.tensor_tensor(pre_s[:, :], hn_s[:, :], bN[:, (u % 2) * P:(u % 2 + 1) * P],
                                ALU.add).then_inc(pre_done, 1)

            def gate_z(t, q, u):
                need(dve, z_done, t + 1)
                v.tensor_tensor(zw_s[:, :], z_s[:, :], w_s[:, u % 2, :], ALU.mult).then_inc(zo_done, 1)

            def one_minus_z(t, q, u):
                need(dve, m_done, t)
                need(dve, z_done, t + 1)
                v.tensor_scalar(omz_s[:, :], z_s[:, :], -1.0, 1.0, ALU.mult, ALU.add).then_inc(omz_done, 1)

            def new_w(t, q, u):
                need(dve, omz_done, t + 1)
                need(dve, n_done, t + 1)
                v.tensor_tensor(m_s[:, :], omz_s[:, :], n_s[:, :], ALU.mult).then_inc(m_done, 1)

            def new_w2(t, q, u):
                need(dve, zo_done, t + 1)
                need(dve, wt_ps, t - 1)
                need(dve, m_done, t + 1)
                v.tensor_tensor(w_s[:, (u + 1) % 2, :], m_s[:, :], zw_s[:, :], ALU.add).then_inc(w_ready, 1)

            def x1(t, q, u):
                need(dve, out_ps, t + 1)
                v.tensor_tensor(at(x_res, t), at(x_res, t), bO[:, 0:P], ALU.add).then_inc(x1_done, 1)

            def stats_b(t, q, u):
                need(dve, x1_done, t + 1)
                if not isinstance(t, int):
                    alone(dve)
                spread_of(lambda t, u: at(x_res, t), st_b, stB)(t, q, u)

            pipeline(dve, T, [(7, gate_n), (3, sum2), (7, gate_n2), (4, rank1), (7, one_minus_z), (3, sum3),
                              (2, mean_rstd(mv_a, rs_a, rsA, hA, nmA)), (10, mean_rstd(mv_b, rs_b, rsB, hB, nmB)),
                              (7, gate_z), (3, sum4), (7, new_w), (4, rank2), (4, scale_adj), (7, new_w2), (3, score_a),
                              (4, rank3), (9, x1), (1, stats_a), (9, stats_b), (1, aggregate(st_a, mv_a, stA, mvA)),
                              (9, aggregate(st_b, mv_b, stB, mvB))])

            steps = [0]

            def grouped(ap):
                return ap.rearrange("p (g b) -> p g b", g=NG)

            def nodes(m, is_last):
                VS = 80
                done = [0]

                def count(ins):
                    done[0] += 1
                    ins.then_inc(s_v, 1)
                    return done[0]

                def after(n):
                    need(dve, s_v, m * VS + n)

                need(dve, s_xp, m + 1)
                xp_bank = bAT[:, :].rearrange("p (b i) -> p i b", i=BLK)
                v.tensor_copy(xp_s[:, 0:1, :], xp_bank[:, 0:1, :]).then_inc(s_xpr, 1)
                evac = count(v.tensor_copy(xp_s[:, 1:BLK, :], xp_bank[:, 1:BLK, :]))
                for k in range(BLK):
                    n = m * BLK + k
                    h_in = h_t[:, n, :] if isinstance(m, int) else \
                        h_t[:, bass.ds(n, 1), :].rearrange("p a b -> p (a b)")
                    need(dve, s_xpr, n + 1)
                    need(dve, s_r2, n + 1)
                    v.tensor_tensor(rx[:, :], rg[:, :], xp_s[:, k, :], ALU.mult).then_inc(s_rx, 1)
                    need(dve, s_z2, n + 1)
                    c_zx = count(v.tensor_tensor(zx[:, k % 2, :], zg[:, :], xp_s[:, k, :], ALU.mult))
                    v.tensor_scalar(omz2[:, k % 2, :], zg[:, :], -1.0, 1.0, ALU.mult, ALU.add).then_inc(s_hcu, 1)
                    after(c_zx)
                    c_zxh = count(v.tensor_tensor(zxh[:, k % 2, :], zx[:, k % 2, :], h_in, ALU.subtract))
                    need(dve, s_hcu, n + 1)
                    need(dve, s_hc, n + 1)
                    c_t1 = count(v.tensor_tensor(t1[:, k % 2, :], omz2[:, k % 2, :], hc[:, :], ALU.mult))
                    if k == 0:
                        need(dve, s_dtp, m)
                        need(dve, s_htp, m)
                    after(max(c_t1, c_zxh))
                    c_dl = count(v.tensor_tensor(dl_s[:, :, k, :], grouped(t1[:, k % 2, :]), grouped(zxh[:, k % 2, :]), ALU.add))
                    if k == BLK - 1:
                        after(c_dl)
                        dve.sem_inc(s_dl, 1)
                    if k < BLK - 1:
                        rest = BLK - 1 - k
                        bank = (bSB, bXA)[k % 2]
                        need(dve, s_cf, m * (BLK - 1) + k + 1)
                        after(c_dl)
                        c_p1 = count(v.tensor_tensor(grouped(p1[:, k % 2, :]), grouped(bank[:, 0:T]), dl_s[:, :, k, :],
                                                     ALU.mult))
                        if k == 0:
                            after(evac)
                        after(c_p1)
                        v.tensor_tensor(xp_s[:, k + 1, :], xp_s[:, k + 1, :], p1[:, k % 2, :], ALU.add).then_inc(s_xpr, 1)
                        if rest > 1:
                            wide = dl_s[:, :, k, :].rearrange("p g (a b) -> p a g b", a=1)\
                                .to_broadcast([P, rest - 1, NG, GB])
                            c_p2 = count(v.tensor_tensor(
                                p2[:, 0:rest - 1, :].rearrange("p i (g b) -> p i g b", g=NG),
                                bank[:, T:rest * T].rearrange("p (i g b) -> p i g b", b=GB, g=NG), wide, ALU.mult))
                            after(c_p2)
                            c_x = count(v.tensor_tensor(xp_s[:, k + 2:BLK, :], xp_s[:, k + 2:BLK, :],
                                                        p2[:, 0:rest - 1, :], ALU.add))
                            after(c_x)
                    h = v.tensor_tensor(hn2[:, :, k, :], grouped(t1[:, k % 2, :]), grouped(zx[:, k % 2, :]), ALU.add)
                    if k < BLK - 1:
                        count(h)
                        h2 = None
                    else:
                        h.then_inc(s_hn, 1)
                    if k < BLK - 1:
                        dve.sem_inc(s_cfu, 1)
                if not is_last:
                    need(dve, s_dtp, m + 1)
                    v.tensor_copy(dt_s[:, :, :], bO[:, :]).then_inc(s_dts, 1)
                while done[0] < VS:
                    dve.sem_inc(s_v, VS - done[0])
                    done[0] = VS

            nodes(0, False)
            with dve.Fori(1, NBLK - 1) as m:
                nodes(m, False)
            nodes(NBLK - 1, True)

            dve.wait_ge(s_xp, NBLK)

            def x2(t, q, u):
                need(dve, q_x2b, t - UN + 1)
                need(dve, q_h2, t - UN + 1)
                need(dve, in_ld[u], 48 * (q + 1))
                v.tensor_tensor(x2_s[:, u, :], at(x_res, t), h_in[:, u, :], ALU.add).then_inc(q_x2, 1)

            def x3(t, q, u):
                need(dve, q_x3h, t - UN + 1)
                need(dve, q_h3, t - UN + 1)
                need(dve, q_x2b, t + 1)
                need(dve, q_w2p, t + 1)
                v.tensor_tensor(x3_s[:, u, :], at(x_res, t), (banks[2], banks[6])[u % 2][:, 0:P],
                                ALU.add).then_inc(q_x3, 1)

            def spread3(i, src, ready):
                def step(t, q, u):
                    need(dve, ready, t + 1)
                    v.bn_stats(st3[:, i, u, :], src[:, u, :]).then_inc(q_st[i], 1)
                return step

            def aggregate3(i):
                return aggregate(st3[:, i, :, :], mv3[:, i, :, :], q_st[i], q_mv[i])

            def finish_a(t, q, u):
                need(dve, q_cvp, t + 1)
                v.tensor_tensor(cb_s[:, u, :], banks[4 + u % 2][:, P:2 * P], brel_bc[:, :], ALU.add).then_inc(q_cb, 1)

            def finish_b(t, q, u):
                need(dve, o_st[u], 16 * q)
                need(dve, q_x3h, t + 1)
                need(dve, q_cb, t + 1)
                v.scalar_tensor_tensor(out=o_s[:, u, :], in0=cb_s[:, u, :], scalar=0.0, in1=at(x_res, t),
                                       op0=ALU.max, op1=ALU.add).then_inc(q_o, 1)

            def nm3(i, h_sem):
                return mean_rstd(mv3[:, i, :, :], rs3[:, i, :, :], q_rs[i], h_sem, q_nm[i])

            pipeline(dve, T, [(7, x3), (1, x2), (2, nm3(0, q_h2)), (8, nm3(1, q_h3)), (11, nm3(2, q_n3)), (15, finish_a),
                              (7, spread3(1, x3_s, q_x3)), (1, spread3(0, x2_s, q_x2)), (10, spread3(2, h3_s, q_h3)),
                              (7, aggregate3(1)), (1, aggregate3(0)), (10, aggregate3(2)), (15, finish_b)])

        @block.tensor
        def _(pe):
            mm, turn = nc.tensor.matmul, nc.tensor.transpose
            pe.wait_ge(s_wload, 16 * (NW - 2))
            pe.wait_ge(s_const, 8)
            for i in range(13):
                ins = turn(banks[i // 4][:, (i % 4) * P:(i % 4 + 1) * P], w_nat[:, i, :], ident[:, :])
                if i % 4 == 3:
                    ins.then_inc(s_wt_ps, 1)
            turn(banks[3][:, P:P + 16], b_nat[:, :], ident[0:16, 0:16]).then_inc(s_wt_ps, 1)
            pe.wait_ge(s_wt_sb, 5)

            def add(out_, l, r, start=False):
                return mm(out_, l, r, start=start, stop=True, skip_group_check=True)

            def turn_adj(t, q, u):
                need(pe, at_sb, t)
                need(pe, adj_in[u], 16 * (q + 1))
                turn(bAT[:, 0:P], adj_s[:, u, :], ident[:, :]).then_inc(at_ps, 1)

            def spread(t, q, u):
                need(pe, adjn_done, t)
                need(pe, sc_done, t + 1)
                need(pe, dv, t * 3 + 3)
                turn(bSB[:, 0:P], score[:, u, :].to_broadcast([P, P]), ident[:, :])
                turn(bSB[:, P:2 * P], dsum[:, u, 3:4].to_broadcast([P, P]), ident[:, :]).then_inc(sb_ps, 1)

            def pick_rows(t, q, u):
                need(pe, xa_sb, t)
                need(pe, hA, t + 1)
                need(pe, at_sb, t + 1)
                need(pe, pick_done, t + 1)
                mm(bXA[:, 0:2 * P], h_a[:, u, :], pa_s[:, u, :, :].rearrange("p c n -> p (c n)"),
                   start=True, stop=True).then_inc(xa_ps, 1)

            def gru_in(t, q, u):
                if u % 2 == 0:
                    return
                two = xa_s[:, u - 1:u + 1, 0:P]
                need(pe, xa_sb, t + 1)
                for bank, done, w in ((bR, r_done, W_IH), (bZ, z_done, W_IH + 1), (bN, pre_done, W_IH + 2)):
                    need(pe, done, t - 1)
                    add(bank[:, 0:2 * P].rearrange("p (c n) -> p c n", c=2), w_t[:, w, :], two, True)

            def gru_state(t, q, u):
                need(pe, w_ready, t + 1)
                c = (u % 2) * P
                add(bR[:, c:c + P], w_t[:, W_HH, :], w_s[:, u % 2, :]).then_inc(r_ps, 1)
                add(bN[:, 2 * P + c:3 * P + c], w_t[:, W_HH + 2, :], w_s[:, u % 2, :]).then_inc(n_ps, 1)
                add(bZ[:, c:c + P], w_t[:, W_HH + 1, :], w_s[:, u % 2, :]).then_inc(z_ps, 1)

            def turn_w(t, q, u):
                need(pe, wn_sb, t)
                need(pe, ht_sb, t - 3)
                need(pe, w_ready, t + 2)
                turn(bW[:, 0:P], w_s[:, (u + 1) % 2, :], ident[:, :]).then_inc(wt_ps, 1)

            def layer0(t, q, u):
                need(pe, x1_done, t)
                need(pe, wn_sb, t + 1)
                mm(bO[:, 0:P], xa_s[:, u, P:2 * P], wn_s[:, u % 2, :], start=True, stop=True).then_inc(out_ps, 1)

            def turn_h(t, q, u):
                need(pe, ht_sb, t)
                need(pe, wn_sb, min(t + 3, T) if isinstance(t, int) else t + 3)
                need(pe, hB, t + 1)
                turn(bW[:, P:2 * P], h_b[:, u, :], ident[:, :]).then_inc(ht_ps, 1)

            pipeline(pe, T, [(7, gru_state), (9, layer0), (5, pick_rows), (4, spread), (2, turn_adj), (11, turn_h),
                             (8, turn_w), (5, gru_in)])

            TERMS = ((0, 0), (0, 1), (1, 0), (0, 2), (1, 1), (2, 0))

            def gather(m, graphs):
                for b in graphs:
                    for i, (c, e) in enumerate(TERMS):
                        if b % GB == 0 and i == 0:
                            need(pe, s_ab, m * NG + b // GB + 1)
                        ins = add(bAT[:, b * BLK:(b + 1) * BLK], hb[:, b, c, :], ab_s[:, b, e, :], b == 0 and i == 0)
                return ins

            def own_part(bank, done, w, m):
                need(pe, done, m * BLK)
                if isinstance(m, int):
                    src = h_t[:, m * BLK:(m + 1) * BLK, :]
                else:
                    alone(pe)
                    src = h_t[:, bass.ds(m * BLK, BLK), :]
                add(bank[:, :], w_t[:, w, :], src.rearrange("p n b -> p (n b)"), True)

            def spread_row(m, k):
                c = m * (BLK - 1) + k
                need(pe, s_cfu, c - 1)
                if k == 0:
                    need(pe, s_cfs, m + 1)
                    if not isinstance(m, int):
                        alone(pe)
                elif not isinstance(m, int):
                    alone(pe)
                bank = (bSB, bXA)[k % 2]
                for i in range(k + 1, BLK):
                    o = (i - k - 1) * T
                    ins = turn(bank[:, o:o + T], cf_s[:, k, i:i + 1].to_broadcast([T, P]), ident[0:T, 0:T])
                ins.then_inc(s_cf, 1)

            pe.wait_ge(hnat, T)
            pe.wait_ge(split_done, T)
            pe.wait_ge(ht_sb, T)
            pe.wait_ge(x1_done, T)
            pe.wait_ge(at_sb, T)
            own_part(bR, s_r2, W_IX, 0)
            own_part(bZ, s_z2, W_IX + 1, 0)
            own_part(bN, s_hc, W_CX, 0)
            gather(0, range(T)).then_inc(s_xp, 1)
            spread_row(0, 0)

            def nodes(m, is_last):
                share = [0, 0, 10, 11, 11, 11, 11, 10]
                b0 = 0
                for k in range(BLK):
                    n = m * BLK + k
                    col = slice(k * T, (k + 1) * T)
                    todo = list(range(b0, b0 + share[k])) if not is_last else []
                    b0 += share[k]
                    need(pe, s_xpr, n + 1)
                    add(bR[:, col], w_t[:, W_IH1, :], xp_s[:, k, :]).then_inc(s_r2p, 1)
                    add(bZ[:, col], w_t[:, W_IH1 + 1, :], xp_s[:, k, :]).then_inc(s_z2p, 1)
                    half = len(todo) // 4
                    if todo:
                        if k == 2:
                            need(pe, s_v, m * 80 + 1)
                            need(pe, s_hrow, 16 * NG * m)
                        gather(m + 1, todo[:half])
                    need(pe, s_rx, n + 1)
                    add(bN[:, col], w_t[:, W_CH, :], rx[:, :]).then_inc(s_c2p, 1)
                    if k < BLK - 2:
                        spread_row(m, k + 1)
                    elif k == BLK - 1 and not is_last:
                        own_part(bR, s_r2, W_IX, m + 1)
                    if todo:
                        gather(m + 1, todo[half:])
                assert b0 == T, b0

                def turn_states():
                    need(pe, s_hts, m)
                    need(pe, s_hn, m + 1)
                    for g in range(NG):
                        ins = turn(bW[:, g * P:(g + 1) * P], hn2[:, g, :, :].rearrange("p k b -> p (k b)"), ident[:, :])
                    ins.then_inc(s_htp, 1)

                if not is_last:
                    need(pe, s_dts, m)
                    need(pe, s_dl, m + 1)
                    for g in range(NG):
                        ins = turn(bO[:, g * P:(g + 1) * P], dl_s[:, g, :, :].rearrange("p k b -> p (k b)"), ident[:, :])
                    ins.then_inc(s_dtp, 1)
                    turn_states()
                    own_part(bZ, s_z2, W_IX + 1, m + 1)
                    need(pe, s_bd, m + 1)
                    need(pe, s_dts, m + 1)
                    for g in range(NG):
                        ins = add(bAT[:, g * P:(g + 1) * P], dt_s[:, g, :],
                                  bd_s[:, g, :, :].rearrange("p b i -> p (b i)"))
                    ins.then_inc(s_xp, 1)
                    own_part(bN, s_hc, W_CX, m + 1)
                    spread_row(m + 1, 0)
                else:
                    turn_states()

            nodes(0, False)
            with pe.Fori(1, NBLK - 1) as m:
                nodes(m, False)
            nodes(NBLK - 1, True)

            pe.wait_ge(s_hts, NBLK)

            def aggregate(t, q, u):
                need(pe, q_ags, t - 1)
                need(pe, q_h2, t + 1)
                need(pe, q_ae, t + 1)
                mm((banks[0], banks[7])[u % 2][:, 0:P], h2_s[:, u, :], ae_s[:, u, :], start=True,
                   stop=True).then_inc(q_agp, 1)

            def mlp_in(t, q, u):
                if u % 2 == 0:
                    return
                need(pe, q_his, t - 1)
                need(pe, q_ags, t + 1)
                two = agg_s[:, u - 1:u + 1, :].rearrange("p a n -> p (a n)")
                mm(banks[1][:, 0:2 * P], w1[:, 0, :], two, start=True, stop=True)
                mm(banks[1][:, 2 * P:4 * P], w1[:, 1, :], two, start=True, stop=True).then_inc(q_hip, 1)

            def mlp_out(t, q, u):
                need(pe, q_x3, t - 1)
                need(pe, q_his, 4 * q + 2 * (u // 2) + 2)
                bank = (banks[2], banks[6])[u % 2]
                col = slice((u % 2) * P, (u % 2 + 1) * P)
                mm(bank[:, 0:P], hid_s[:, u // 2, 0, col], w2[:, 0, :], start=True, stop=False)
                mm(bank[:, 0:P], hid_s[:, u // 2, 1, col], w2[:, 1, :], start=False, stop=True).then_inc(q_w2p, 1)

            def turn_n3(t, q, u):
                need(pe, q_g3, t)
                need(pe, q_n3, t + 1)
                turn(banks[3][:, 0:P], n3_s[:, u, :], ident[:, :]).then_inc(q_n3p, 1)

            def rel_root(t, q, u):
                need(pe, q_cb, t - 1)
                need(pe, q_g3, t + 1)
                add(banks[4 + u % 2][:, 0:2 * P], g3_s[:, u, :], wrr[:, :, :].rearrange("p c n -> p (c n)"),
                    True).then_inc(q_y1p, 1)

            def conv(t, q, u):
                need(pe, q_y1, t + 1)
                need(pe, ac_ld[u], 16 * (q + 1))
                add(banks[4 + u % 2][:, P:2 * P], ac_in[:, u, :], y1_s[:, u, :]).then_inc(q_cvp, 1)

            pipeline(pe, T, [(7, mlp_out), (4, aggregate), (15, conv), (13, turn_n3), (5, mlp_in), (14, rel_root)])


_INS = ['x', 'adj', 'L0_gnn_pool_p', 'L0_gnn_W_ih', 'L0_gnn_W_hh', 'L0_gnn_b_ih', 'L0_gnn_b_hh', 'L0_gnn_W0',
        'L1_gnn_W_ioux', 'L1_gnn_b_ioux', 'L1_gnn_W_iouh', 'L1_gnn_b_iouh', 'L1_gnn_W_coux', 'L1_gnn_b_coux',
        'L1_gnn_W_couh', 'L1_gnn_b_couh', 'L2_gnn_eps', 'L2_gnn_W1', 'L2_gnn_b1', 'L2_gnn_W2', 'L2_gnn_b2',
        'L3_gnn_W_rel', 'L3_gnn_b_rel', 'L3_gnn_W_root', 'L3_gnn_ln_gamma', 'L3_gnn_ln_beta']


def kernel(**inputs):
    import numpy as _np
    import concourse.bacc as _bacc
    from concourse import mybir as _mybir
    from concourse.bass_utils import run_bass_kernel_spmd as _run

    nc = _bacc.Bacc("TRN2", target_bir_lowering=False, num_devices=1)
    arrays, dram = {}, {}
    for name in _INS:
        a = _np.ascontiguousarray(inputs[name])
        arrays[f"in_{name}_dram"] = a
        dram[name] = nc.dram_tensor(f"in_{name}_dram", a.shape, _mybir.dt.from_np(a.dtype), kind="ExternalInput").ap()
    out = nc.dram_tensor("out_0_dram", inputs["x"].shape, _mybir.dt.float32, kind="ExternalOutput").ap()
    graph_layers(nc, dram, out)
    r = _run(nc, [arrays], core_ids=[0])
    return r.results[0]["out_0_dram"]
```

```python
from contextlib import ExitStack

import concourse.bass as bass
from concourse import mybir

F32 = mybir.dt.float32
BF16 = mybir.dt.bfloat16
ALU = mybir.AluOpType
ACT = mybir.ActivationFunctionType
AX_X = mybir.AxisListType.X

P = 128
UN = 4
BLK = 8
GB = P // BLK
PRO = 24
LN_EPS = 1e-5


def need(eng, sem, count):
    if isinstance(count, int) and count <= 0:
        return
    eng.wait_ge(sem, count)


def pipeline(eng, total, steps):
    last = max(lag for lag, _ in steps)

    def one(s, su, q):
        for lag, step in steps:
            if q is None:
                t = s - lag
                if 0 <= t < total:
                    step(t, t // UN, t % UN)
            else:
                step(q * UN + (su - lag), q + (su - lag) // UN, (su - lag) % UN)

    for s in range(PRO):
        one(s, 0, None)
    with eng.Fori(PRO // UN // 2, total // UN // 2) as trip:
        for su in range(2 * UN):
            one(None, su, trip * 2)
    for s in range(total, total + last):
        one(s, 0, None)


def blocks(eng, count, nodes):
    nodes(0, 0, False)
    with eng.Fori(0, count // 2 - 1) as j:
        nodes(j * 2 + 1, 1, False)
        nodes(j * 2 + 2, 0, False)
    nodes(count - 1, 1, True)


def pairs(q, u):
    return q * 2 + u // 2 + 1


def at(tile, t):
    if isinstance(t, int):
        return tile[:, t, :]
    return tile[:, bass.ds(t, 1), :].rearrange("p a d -> p (a d)")


def rows(tensor, t):
    if isinstance(t, int):
        return tensor[t, :, :]
    return tensor[bass.ds(t, 1), :, :].rearrange("a n m -> n (a m)")


def part(tile, t, c):
    if isinstance(t, int):
        return tile[:, t, c, :]
    return tile[:, bass.ds(t, 1), c, :].rearrange("p a d -> p (a d)")


def graph_layers(nc, d, out):
    x, adj = d["x"], d["adj"]
    T, N, D = x.shape
    NBLK = N // BLK
    NG = T // GB
    assert N == P and D == P and T * BLK == 512

    at_scr = nc.dram_tensor("at_scr", (T, N, N), F32, kind="Internal").ap()
    an_scr = nc.dram_tensor("an_scr", (T, N, N), F32, kind="Internal").ap()
    x1_scr = nc.dram_tensor("x1_scr", (T, N, D), F32, kind="Internal").ap()
    c_scr = nc.dram_tensor("c_scr", (NBLK, BLK, BLK, T), F32, kind="Internal").ap()
    h_scr = nc.dram_tensor("h_scr", (N, T, D), F32, kind="Internal").ap()

    with ExitStack() as ctx:
        def sb(name, shape):
            return ctx.enter_context(nc.sbuf_tensor(name, shape, F32))

        def sem(name):
            return ctx.enter_context(nc.semaphore(name))

        banks = [ctx.enter_context(nc.psum_tensor(f"bank{i}", [P, 512], F32)) for i in range(8)]

        ident = sb("ident", [P, P])
        below = sb("below", [P, P])
        iota = sb("iota", [P, P])
        diag16 = sb("diag16", [P, GB])
        mhalf = sb("mhalf", [P, 2])
        epsc = sb("epsc", [P, 2])
        w_nat = sb("w_nat", [P, 13, P])
        w_t = sb("w_t", [P, 13, P])
        w1 = sb("w1", [P, 2, P])
        w2 = sb("w2", [P, 2, P])
        wrr = sb("wrr", [P, 2, P])
        p_bc = sb("p_bc", [P, P])
        b2_bc = sb("b2_bc", [P, P])
        brel_bc = sb("brel_bc", [P, P])
        b_nat = sb("b_nat", [16, P])
        bcol = sb("bcol", [P, 16])
        bias = sb("bias", [P, 8])
        eps1 = sb("eps1", [P, 1])
        eye_eps = sb("eye_eps", [P, P])
        junk = sb("junk", [P, 3, P])
        pn2 = sb("pn2", [P, 1])
        rpn = sb("rpn", [P, 1])

        adjb_f = sb("adjb_f", [P, T, 3 * N // 2])
        hb_f = sb("hb_f", [P, T, 3 * D // 2])
        adjb = adjb_f[:, :, :].bitcast(BF16).rearrange("p t (c n) -> p t c n", c=3)
        hb = hb_f[:, :, :].bitcast(BF16).rearrange("p t (c n) -> p t c n", c=3)
        x_res = hb_f[:, :, 0:D]
        h_t = sb("h_t", [P, N, T])
        coef = sb("coef", [T, NBLK, BLK, BLK])
        next_r = sb("next_r", [P, NBLK - 1, NG, BLK])

        adj_s = sb("adj_s", [P, UN, N])
        slots1 = sb("slots1", [P, UN, 4, P])
        pa_s = slots1[:, :, 0:2, :]
        an_s = sb("an_s", [P, UN, N])
        ra_s, rh_s = slots1[:, :, 2, :], slots1[:, :, 3, :]
        st_a = sb("st_a", [P, UN, 6])
        mv_a = sb("mv_a", [P, UN, 2])
        rs_a = sb("rs_a", [P, UN, 3])
        h_a = sb("h_a", [P, UN, D])
        score = sb("score", [P, UN, 1])
        th = sb("th", [P, UN, 1])
        dsum = sb("dsum", [P, UN, 4])
        cnt = sb("cnt", [P, UN, 4])
        xa_s = sb("xa_s", [P, UN, 2 * P])
        w_s = sb("w_s", [P, 2, P])
        r_s = sb("r_s", [P, P])
        z_s = sb("z_s", [P, P])
        n_s = sb("n_s", [P, P])
        hn_s = sb("hn_s", [P, P])
        pre_s = sb("pre_s", [P, P])
        zw_s = sb("zw_s", [P, P])
        omz_s = sb("omz_s", [P, P])
        m_s = sb("m_s", [P, P])
        wn_s = sb("wn_s", [P, 2, P])
        st_b = sb("st_b", [P, UN, 6])
        mv_b = sb("mv_b", [P, UN, 2])
        rs_b = sb("rs_b", [P, UN, 3])
        h_b = sb("h_b", [P, UN, D])

        s_const = sem("const_ready")
        s_wload, s_wload3 = sem("weights_loaded"), sem("stage3_weights_loaded")
        s_xload = [sem("x_head_loaded"), sem("x_rest_loaded")]
        s_wt_ps = sem("w_turned")
        s_wt_sb = sem("w_turned_copied")
        s_setp = sem("setup_vector_step")
        s_rpn = sem("pool_norm_ready")
        s_alone = sem("lone_wait")

        adj_in = [sem(f"adj_in{i}") for i in range(UN)]
        at_out = [sem(f"at_out{i}") for i in range(UN)]
        s_anout = [sem(f"adjn_stored{i}") for i in range(UN)]
        x1_out = [sem(f"x1_stored{i}") for i in range(UN)]
        s_coef = sem("coef_loaded")
        at_ps, at_sb = sem("at_turned"), sem("at_copied")
        stA, mvA, rsA0, rsA = sem("stats_a"), sem("mean_var_a"), sem("var_eps_a"), sem("rstd_a")
        nmA, hA = sem("mean_rstd_a"), sem("h_a_ready")
        sc_done, th_done = sem("score_ready"), sem("tanh_score_ready")
        sum_done, dv = sem("row_sum_ready"), sem("row_sum_steps")
        sb_ps = sem("score_dinv_spread")
        rk, pick_done = sem("rank_steps"), sem("pick_ready")
        adjn_done = sem("adjn_ready")
        xa_ps, xa_sb = sem("xa_product"), sem("xa_copied")
        r_ps, z_ps, n_ps = sem("r_gate_sum"), sem("z_gate_sum"), sem("n_gate_sum")
        r_done, z_done, n_done = sem("r_ready"), sem("z_ready"), sem("n_ready")
        hn_done, pre_done, zo_done, m_done, w_ready, omz_done = (sem("hn_scaled"), sem("n_input_ready"), sem("zw_ready"),
                                                       sem("omz_n_ready"), sem("w_ready"), sem("omz_ready"))
        wt_ps, wn_sb = sem("w_new_turned"), sem("w_new_copied")
        out_ps, x1_done = sem("layer0_product"), sem("x1_ready")
        a1_done, ra_done, a2_done, split_done = (sem("adj_part1"), sem("adj_rest"), sem("adj_part2"),
                                                 sem("adj_part3"))
        h1_done, rh_done, h2_done = sem("h_part1"), sem("h_rest"), sem("h_part2")
        stB, mvB, rsB0, rsB = sem("stats_b"), sem("mean_var_b"), sem("var_eps_b"), sem("rstd_b")
        nmB, hB, hnat = sem("mean_rstd_b"), sem("h_b_ready"), sem("h_part3")
        ht_ps, ht_sb = sem("h_b_turned"), sem("h_t_ready")

        bR, bZ, bN, bAT, bSB, bXA, bW, bO = banks

        W_IH, W_HH, W_0, W_IX, W_IH1, W_CX, W_CH = 0, 3, 6, 7, 9, 11, 12

        def alone(eng):
            eng.sem_inc(s_alone, 1)

        xp_s = sb("xp_s", [P, BLK, T])
        rg = sb("rg", [P, T])
        zg = sb("zg", [P, T])
        hc = sb("hc", [P, T])
        rx = sb("rx", [P, T])
        zx = sb("zx", [P, 2, T])
        omz2 = sb("omz2", [P, 2, T])
        zxh = sb("zxh", [P, 2, T])
        t1 = sb("t1", [P, 2, T])
        c_omz = sb("c_omz", [P, 2, T])
        c_zxh = sb("c_zxh", [P, 2, T])
        xp_a = sb("xp_a", [P, 2, T])
        p1 = sb("p1", [P, 2, T])
        p2 = sb("p2", [P, BLK, T])
        dl_s = sb("dl_s", [P, NG, BLK, GB])
        hn2 = sb("hn2", [P, NG, BLK, GB])
        cf_flat = slots1[:, :, :, :].rearrange("p u c n -> p (u c n)")
        cf_first = [sum(BLK - 1 - i for i in range(k)) * T for k in range(BLK)]
        cf_turned = an_s[:, :, :].rearrange("p u n -> p (u n)")

        def cf(k, i):
            o = cf_first[k] + (i - k - 1) * T
            return cf_flat[:, o:o + T]

        bd_s = sb("bd_s", [P, NG, GB, BLK])
        dt_s = sb("dt_s", [P, NG, P])
        hnt_s = sb("hnt_s", [P, NG, P])
        hrest = sb("hrest", [P, NG, P])
        hntb = xa_s[:, :, :].rearrange("p u n -> p (u n)")[:, 0:NG * 3 * P // 2].bitcast(BF16)            .rearrange("p (g c d) -> p g c d", c=3, g=NG)
        ab_s = w_nat[:, :, :].rearrange("p i k -> p (i k)")[:, 0:T * 3 * BLK // 2].bitcast(BF16)            .rearrange("p (t c i) -> p t c i", c=3, t=T)

        s_xp = sem("xp_bank_full")
        s_xpr = sem("xp_ready")
        s_r2p, s_z2p, s_c2p = sem("r2_sum"), sem("z2_sum"), sem("c2_sum")
        s_r2, s_z2, s_hc, s_rx = sem("r2_ready"), sem("z2_ready"), sem("hc_ready"), sem("rx_ready")
        s_v = sem("vector_steps")
        s_hcu = sem("one_minus_z_ready")
        s_cf = sem("coef_rows_loaded")
        s_cfu = sem("coef_row_used")
        s_ctp, s_cts, s_cst = sem("coef_turned"), sem("coef_copied"), sem("coef_stored")
        s_nextr = sem("next_rows_loaded")
        s_dl = sem("block_changes_ready")
        s_hn = sem("block_states_ready")
        s_dtp, s_dts = sem("changes_turned"), sem("changes_copied")
        s_dtp2, s_dts2 = sem("changes_turned_2"), sem("changes_copied_2")
        VS = 112
        r_banks, z_banks = (bR, bSB), (bZ, bXA)
        s_htp, s_hts = sem("states_turned"), sem("states_copied")
        s_bd = sem("block_diag_ready")
        s_hscr = sem("states_stored")
        s_h1, s_hr, s_h2, s_h3 = sem("states_part1"), sem("states_rest"), sem("states_part2"), sem("states_part3")
        s_hrow = sem("part_rows_stored")
        s_ab = sem("next_adjacency_ready")

        taken = [0]
        slot_space = adjb_f[:, :, :].rearrange("p t c -> p (t c)")

        def slots(width=1):
            first = taken[0]
            taken[0] += UN * width
            return slot_space[:, first * P:taken[0] * P].rearrange("p (u n) -> p u n", u=UN)

        st3 = sb("st3", [P, 3, UN, 6])
        mv3 = sb("mv3", [P, 3, UN, 2])
        rs3 = sb("rs3", [P, 3, UN, 3])
        ae_in, ac_in, ae_s = slots(), slots(), slots()
        x2_s, h2_s, agg_s, hid_s = slots(), slots(), slots(), slots(2)
        hid_s = hid_s.rearrange("p (a c) n -> p a c n", c=2)
        x3_s, h3_s, n3_s, g3_s = slots(), slots(), slots(), slots()
        h_in = slots()
        y1_s, cb_s, o_s = slots(), slots(), h_t[:, 0:2 * UN, :].rearrange("p (u c) n -> p u (c n)", u=UN)

        in_ld = [sem(f"graph_in{i}") for i in range(UN)]
        ac_ld = [sem(f"ac_ld{i}") for i in range(UN)]
        o_st = [sem(f"o_st{i}") for i in range(UN)]
        q_x2, q_ae = sem("x2_ready"), sem("adj_eps_ready")
        q_st = [sem(f"q_st{i}") for i in range(3)]
        q_mv = [sem(f"q_mv{i}") for i in range(3)]
        q_ve = [sem(f"q_ve{i}") for i in range(3)]
        q_rs = [sem(f"q_rs{i}") for i in range(3)]
        q_nm = [sem(f"q_nm{i}") for i in range(3)]
        q_h2 = sem("h2_ready")
        q_x2b = sem("x2b_ready")
        q_agp, q_ags = sem("agg_product"), sem("agg_copied")
        q_hip, q_his = sem("hidden_product"), sem("hidden_ready")
        q_w2p, q_x3 = sem("w2_product"), sem("x3_ready")
        q_h3, q_x3h, q_n3 = sem("h3_ready"), sem("x3h_ready"), sem("n3_ready")
        q_n3p, q_g3 = sem("n3_turned"), sem("g3_ready")
        q_y1p, q_y1, q_cvp = sem("y1_product"), sem("y1_copied"), sem("conv_product")
        q_cb, q_o = sem("conv_biased"), sem("out_ready")

        X_LOADS = (T - PRO) // UN
        NW, NW3 = 17, 7
        block = ctx.enter_context(nc.Block())

        @block.sync
        def _(sp):
            sp.dma_start(x_res[:, 0:PRO, :], x[0:PRO, :, :].rearrange("t n d -> n t d")).then_inc(s_xload[0], 16)
            loads = [0]

            def w(dst, src):
                sp.dma_start(dst, src).then_inc(s_wload, 16)
                loads[0] += 1

            for i, name in ((W_IH, "L0_gnn_W_ih"), (W_HH, "L0_gnn_W_hh"), (W_IX, "L1_gnn_W_ioux"),
                            (W_IH1, "L1_gnn_W_iouh"), (W_CX, "L1_gnn_W_coux"), (W_CH, "L1_gnn_W_couh")):
                c = d[name].shape[0] // P
                w(w_nat[:, i:i + c, :], d[name].rearrange("(c p) k -> p c k", p=P))
            w(w_nat[:, W_0, :], d["L0_gnn_W0"].rearrange("a p k -> (a p) k"))
            w(p_bc[:, :], d["L0_gnn_pool_p"].partition_broadcast(P))
            c0 = 0
            for name in ("L0_gnn_b_ih", "L0_gnn_b_hh", "L1_gnn_b_ioux", "L1_gnn_b_iouh", "L1_gnn_b_coux",
                         "L1_gnn_b_couh", "L2_gnn_b1", "L3_gnn_ln_gamma", "L3_gnn_ln_beta"):
                c = d[name].shape[0] // P
                w(b_nat[c0:c0 + c, :], d[name].rearrange("(c p) -> c p", p=P))
                c0 += c
            assert loads[0] == NW, loads
            def load_rest(t, q, u):
                if isinstance(t, int) and PRO + t * UN < T:
                    some = slice(PRO + t * UN, PRO + (t + 1) * UN)
                    sp.dma_start(x_res[:, some, :], x[some, :, :].rearrange("t n d -> n t d")).then_inc(s_xload[1], 16)
                if isinstance(t, int) and t == PRO - 1:
                    load_late()

            def load_late():
                for dst, src in ((w1[:, :, :], d["L2_gnn_W1"].rearrange("p (c k) -> p c k", c=2)),
                                 (w2[:, :, :], d["L2_gnn_W2"].rearrange("(c p) k -> p c k", p=P)),
                                 (wrr[:, 0, :], d["L3_gnn_W_rel"]), (wrr[:, 1, :], d["L3_gnn_W_root"]),
                                 (b2_bc[:, :], d["L2_gnn_b2"].partition_broadcast(P)),
                                 (brel_bc[:, :], d["L3_gnn_b_rel"].partition_broadcast(P)),
                                 (eps1[:, :], d["L2_gnn_eps"].partition_broadcast(P))):
                    sp.dma_start(dst, src).then_inc(s_wload3, 16)

            def load_adj(t, q, u):
                need(sp, at_ps, t - UN + 1)
                need(sp, sum_done, t - UN + 1)
                need(sp, adjn_done, t - UN + 1)
                src = rows(adj, t)
                sp.dma_start(adj_s[:, u, :], src).then_inc(adj_in[u], 16)

            def store_at(t, q, u):
                need(sp, at_sb, t + 1)
                dst = rows(at_scr, t)
                sp.dma_start(dst, pa_s[:, u, 1, :]).then_inc(at_out[u], 16)

            def store_adjn(t, q, u):
                need(sp, adjn_done, t + 1)
                dst = rows(an_scr, t)
                sp.dma_start(dst, an_s[:, u, :]).then_inc(s_anout[u], 16)

            def store_x1(t, q, u):
                need(sp, h1_done, t - UN + 1)
                if not isinstance(t, int):
                    alone(sp)
                need(sp, x1_done, t + 1)
                sp.dma_start(rows(x1_scr, t), at(x_res, t)).then_inc(x1_out[u], 16)

            pipeline(sp, T, [(0, load_adj), (0, load_rest), (4, store_at), (6, store_adjn), (11, store_x1)])

            for u in range(UN):
                sp.wait_ge(s_anout[u], 16 * (T // UN))
            piece = bass.AP(an_scr.tensor, 0, [[N * N, T], [BLK * N + BLK, NBLK], [N, BLK], [1, BLK]])
            for k in range(BLK):
                sp.dma_start(coef[:, :, k, :], piece[:, :, k, :]).then_inc(s_coef, 16)
            sp.wait_ge(s_cts, 1)
            rows_of = bass.AP(c_scr.tensor, 0, [[T, P], [P * T, NBLK // 2], [1, T]])
            sp.dma_start(rows_of, cf_turned.rearrange("p (c b) -> p c b", b=T)).then_inc(s_cst, 16)
            for u in range(UN):
                sp.wait_ge(at_out[u], 16 * (T // UN))
            sp.wait_ge(hnat, T)
            sp.wait_ge(split_done, T)
            sp.wait_ge(s_cst, 16)

            def load_coef_row(m, k):
                src = bass.AP(c_scr.tensor, ((m * BLK + k) * BLK + k + 1) * T, [[0, P], [1, (BLK - 1 - k) * T]])
                sp.dma_start(cf_flat[:, cf_first[k]:cf_first[k + 1]], src).then_inc(s_cf, 16)

            for k in range(BLK - 1):
                load_coef_row(0, k)
            for g in range(NG):
                for k in range(BLK):
                    src = bass.AP(an_scr.tensor, g * N * N + k * N + BLK,
                                  [[NG * N * N, GB], [BLK * N + BLK, NBLK - 1], [1, BLK]])
                    sp.dma_start(next_r[k * GB:(k + 1) * GB, :, g, :], src).then_inc(s_nextr, 16)

            for m in range(NBLK):
                if m < NBLK - 1:
                    for k in range(BLK - 1):
                        sp.wait_ge(s_cfu, m * (BLK - 1) + k + 1)
                        load_coef_row(m + 1, k)
                sp.wait_ge(s_hts, m + 1)
                own_rows = slice(m * BLK, (m + 1) * BLK)
                sp.dma_start(h_scr[own_rows, :, :].rearrange("k (b g) d -> k b (g d)", g=NG),
                             hnt_s[:, :, :].rearrange("p g d -> p (g d)")).then_inc(s_hscr, 16)
                if m < NBLK - 1:
                    sp.wait_ge(s_h3, m + 1)
                    sp.dma_start(hb[own_rows, :, :, :].rearrange("k (b g) c d -> k b (g c d)", g=NG),
                                 hntb[:, :, :, :].rearrange("p g c d -> p (g c d)")).then_inc(s_hrow, 16)

            def load_ae(t, q, u):
                need(sp, q_ae, t - UN + 1)
                src = rows(at_scr, t)
                sp.dma_start(ae_in[:, u, :], src).then_inc(in_ld[u], 16)

            def load_x(t, q, u):
                need(sp, q_x2, t - UN + 1)
                sp.dma_start(h_in[:, u, :], h_scr[:, t, :] if isinstance(t, int) else
                             h_scr[:, bass.ds(t, 1), :].rearrange("n a d -> n (a d)")).then_inc(in_ld[u], 16)
                sp.dma_start(at(x_res, t), rows(x1_scr, t)).then_inc(in_ld[u], 16)

            def load_ac(t, q, u):
                need(sp, q_cvp, t - UN + 1)
                src = rows(at_scr, t)
                sp.dma_start(ac_in[:, u, :], src).then_inc(ac_ld[u], 16)

            def store_out(t, q, u):
                need(sp, q_o, t + 1)
                dst = rows(out, t)
                sp.dma_start(dst, o_s[:, u, :]).then_inc(o_st[u], 16)

            for u in range(UN):
                sp.wait_ge(x1_out[u], 16 * (T // UN))
            sp.wait_ge(s_hscr, 16 * NBLK)
            sp.wait_ge(s_hrow, 16 * (NBLK - 1))
            sp.wait_ge(s_xp, NBLK)
            pipeline(sp, T, [(0, load_x), (0, load_ae), (14, load_ac), (18, store_out)])
            for u in range(UN):
                sp.wait_ge(o_st[u], 16 * (T // UN))

        @block.gpsimd
        def _(pool):
            g = nc.gpsimd
            g.memset(mhalf[:, :], -0.5).then_inc(s_const, 1)
            g.memset(epsc[:, :], LN_EPS).then_inc(s_const, 1)
            g.memset(ident[:, :], 0.0).then_inc(s_const, 1)
            g.memset(below[:, :], 1.0).then_inc(s_const, 1)
            g.memset(diag16[:, :], 0.0).then_inc(s_const, 1)
            pool.wait_ge(s_const, 5)
            g.affine_select(out=ident[:, :], in_=ident[:, :], compare_op=ALU.not_equal, fill=1.0, base=0,
                            pattern=[[-1, P]], channel_multiplier=1).then_inc(s_const, 1)
            g.affine_select(out=below[:, :], in_=below[:, :], compare_op=ALU.is_gt, fill=0.0, base=0,
                            pattern=[[-1, P]], channel_multiplier=1).then_inc(s_const, 1)
            g.iota(iota[:, :], pattern=[[1, P]], base=0, channel_multiplier=0,
                   allow_small_or_imprecise_dtypes=True).then_inc(s_const, 1)
            for k in range(BLK):
                pool.wait_ge(s_const, 8 + k)
                g.affine_select(out=diag16[:, :], in_=diag16[:, :], compare_op=ALU.not_equal, fill=1.0,
                                base=-GB * k, pattern=[[-1, GB]], channel_multiplier=1).then_inc(s_const, 1)
            pool.wait_ge(s_setp, 1)
            g.tensor_tensor(rpn[:, :], pn2[:, :], mhalf[:, 0:1], ALU.pow).then_inc(s_rpn, 1)

            def rstd(mv, ve_sem, mv_sem, out_sem, rs):
                def step(t, q, u):
                    if u % 2 == 0:
                        return
                    two = slice(u - 1, u + 1)
                    need(pool, mv_sem, t + 1)
                    g.tensor_tensor(rs[:, two, 0:1], mv[:, two, 1:2], epsc[:, 0:2].rearrange("p (a b) -> p a b", b=1),
                                    ALU.add).then_inc(ve_sem, 1)
                    need(pool, ve_sem, pairs(q, u))
                    g.tensor_tensor(rs[:, two, 1:2], rs[:, two, 0:1], mhalf[:, 0:2].rearrange("p (a b) -> p a b", b=1),
                                    ALU.pow).then_inc(out_sem, 1)
                return step

            def rest(done, whole, left, parts, i, out_sem):
                def step(t, q, u):
                    if i == 0:
                        need(pool, split_done if parts is adjb else hnat, t - UN + 1)
                    need(pool, done, t + 1)
                    if not isinstance(t, int):
                        alone(pool)
                    dst = left[:, u, :] if i == 0 else part(parts, t, 2)
                    g.tensor_tensor(dst, whole[:, u, :], part(parts, t, i), ALU.subtract).then_inc(out_sem, 1)
                return step

            def one_minus_z(t, q, u):
                need(pool, m_done, t)
                need(pool, z_done, t + 1)
                if not isinstance(t, int):
                    alone(pool)
                g.tensor_scalar(omz_s[:, :], z_s[:, :], -1.0, 1.0, ALU.mult, ALU.add).then_inc(omz_done, 1)

            def gate_z(t, q, u):
                need(pool, w_ready, t + 1)
                g.tensor_tensor(zw_s[:, :], z_s[:, :], w_s[:, u % 2, :], ALU.mult).then_inc(zo_done, 1)

            pipeline(pool, T, [(8, one_minus_z), (8, gate_z), (2, rstd(mv_a, rsA0, mvA, rsA, rs_a)),
                               (11, rstd(mv_b, rsB0, mvB, rsB, rs_b)), (7, rest(a1_done, an_s, ra_s, adjb, 0, ra_done)),
                               (9, rest(a2_done, ra_s, None, adjb, 1, split_done)),
                               (15, rest(h1_done, h_b, rh_s, hb, 0, rh_done)),
                               (17, rest(h2_done, rh_s, None, hb, 1, hnat))])

            pool.wait_ge(s_nextr, 16 * NG * BLK)

            def block_work(m):
                need(pool, s_xp, m + 1)
                if isinstance(m, int):
                    row = next_r[:, m, :, :]
                else:
                    row = next_r[:, bass.ds(m, 1), :, :].rearrange("p a g i -> p (a g) i")
                    alone(pool)
                for gg in range(NG):
                    last = g.tensor_tensor(bd_s[:, gg, :, :], row[:, gg:gg + 1, :].to_broadcast([P, GB, BLK]),
                                           diag16[:, :].rearrange("p (b a) -> p b a", a=1).to_broadcast([P, GB, BLK]),
                                           ALU.mult)
                last.then_inc(s_bd, 1)

            def split_states(m):
                need(pool, s_h1, m + 1)
                g.tensor_tensor(hrest[:, :, :], hnt_s[:, :, :], hntb[:, :, 0, :], ALU.subtract).then_inc(s_hr, 1)
                need(pool, s_h2, m + 1)
                g.tensor_tensor(hntb[:, :, 2, :], hrest[:, :, :], hntb[:, :, 1, :], ALU.subtract).then_inc(s_h3, 1)

            block_work(0)
            with pool.Fori(1, NBLK - 1) as m:
                split_states(m - 1)
                block_work(m)
            split_states(NBLK - 2)

            pool.wait_ge(s_setp, 4)

            def adj_eps(t, q, u):
                need(pool, q_agp, t - UN + 1)
                need(pool, in_ld[u], 48 * (q + 1))
                g.tensor_tensor(ae_s[:, u, :], ae_in[:, u, :], eye_eps[:, :], ALU.add).then_inc(q_ae, 1)

            def x2b(t, q, u):
                need(pool, q_x2, t + 1)
                if not isinstance(t, int):
                    alone(pool)
                g.tensor_tensor(at(x_res, t), x2_s[:, u, :], b2_bc[:, :], ALU.add).then_inc(q_x2b, 1)

            def r3(i):
                return rstd(mv3[:, i, :, :], q_ve[i], q_mv[i], q_rs[i], rs3[:, i, :, :])

            pipeline(pool, T, [(1, adj_eps), (1, x2b), (1, r3(0)), (11, r3(2)), (8, r3(1))])

        @block.scalar
        def _(act):
            a = nc.scalar
            a.preload_act_table_set("sigmoid_and_others")
            for c in range(4):
                n = min(4, 13 - 4 * c)
                act.wait_ge(s_wt_ps, c + 1)
                a.activation(w_t[:, 4 * c:4 * c + n, :], banks[c][:, 0:n * P], ACT.Copy).then_inc(s_wt_sb, 1)
            a.activation(bcol[:, :], banks[3][:, P:P + 16], ACT.Copy).then_inc(s_wt_sb, 1)
            act.wait_ge(s_wt_sb, 5)
            a.activation(w_s[:, 0, :], w_t[:, W_0, :], ACT.Copy).then_inc(w_ready, 1)
            act.wait_ge(s_setp, 2)
            act.wait_ge(s_rpn, 1)

            def sig_r(t, q, u):
                need(act, r_ps, t + 1)
                need(act, hn_done, t)
                a.activation(r_s[:, :], bR[:, 0:P], ACT.Sigmoid, bias=bias[:, 0:1]).then_inc(r_done, 1)

            def sig_z(t, q, u):
                need(act, z_ps, t + 1)
                need(act, zo_done, t)
                a.activation(z_s[:, :], bZ[:, 0:P], ACT.Sigmoid,
                             bias=bias[:, 1:2]).then_inc(z_done, 1)

            def tanh_n(t, q, u):
                need(act, pre_done, t + 1)
                need(act, m_done, t)
                a.activation(n_s[:, :], pre_s[:, :], ACT.Tanh, bias=bcol[:, 2:3]).then_inc(n_done, 1)

            def copy_at(t, q, u):
                need(act, at_out[u], 16 * q)
                need(act, xa_ps, t - UN + 1)
                need(act, at_ps, t + 1)
                a.activation(pa_s[:, u, 1, :], bAT[:, 0:P], ACT.Copy).then_inc(at_sb, 1)

            def relu_a(t, q, u):
                need(act, xa_ps, t - UN + 1)
                need(act, nmA, q * 2 + u // 2 + 1)
                a.activation(h_a[:, u, :], at(x_res, t), ACT.Relu, bias=rs_a[:, u, 2:3],
                             scale=rs_a[:, u, 1:2]).then_inc(hA, 1)

            def tanh_score(t, q, u):
                need(act, pick_done, t - UN + 1)
                need(act, sc_done, t + 1)
                a.activation(th[:, u, :], score[:, u, :], ACT.Tanh, scale=rpn[:, 0:1]).then_inc(th_done, 1)

            def copy_xa(t, q, u):
                need(act, out_ps, t - UN + 1)
                need(act, xa_ps, t + 1)
                a.activation(xa_s[:, u, :], bXA[:, 0:2 * P], ACT.Copy).then_inc(xa_sb, 1)

            def copy_wn(t, q, u):
                need(act, out_ps, t - 1)
                need(act, wt_ps, t + 1)
                a.activation(wn_s[:, u % 2, :], bW[:, 0:P], ACT.Copy).then_inc(wn_sb, 1)

            def relu_b(t, q, u):
                need(act, rh_done, t - UN + 1)
                need(act, ht_ps, t - UN + 1)
                need(act, nmB, q * 2 + u // 2 + 1)
                a.activation(h_b[:, u, :], at(x_res, t), ACT.Relu, bias=rs_b[:, u, 2:3],
                             scale=rs_b[:, u, 1:2]).then_inc(hB, 1)

            def split_h1(t, q, u):
                need(act, x1_out[u], 16 * (q + 1))
                need(act, hB, t + 1)
                if not isinstance(t, int):
                    alone(act)
                a.activation(part(hb, t, 0), h_b[:, u, :], ACT.Copy).then_inc(h1_done, 1)

            def split_a1(t, q, u):
                need(act, adjn_done, t + 1)
                if not isinstance(t, int):
                    alone(act)
                a.activation(part(adjb, t, 0), an_s[:, u, :], ACT.Copy).then_inc(a1_done, 1)

            def split_a2(t, q, u):
                need(act, ra_done, t + 1)
                if not isinstance(t, int):
                    alone(act)
                a.activation(part(adjb, t, 1), ra_s[:, u, :], ACT.Copy).then_inc(a2_done, 1)

            def split_h2(t, q, u):
                need(act, rh_done, t + 1)
                if not isinstance(t, int):
                    alone(act)
                a.activation(part(hb, t, 1), rh_s[:, u, :], ACT.Copy).then_inc(h2_done, 1)

            def copy_ht(t, q, u):
                need(act, wt_ps, min(t + 6, T) if isinstance(t, int) else t + 6)
                need(act, ht_ps, t + 1)
                if isinstance(t, int):
                    dst = h_t[:, :, t:t + 1]
                else:
                    alone(act)
                    dst = h_t[:, :, bass.ds(t, 1)]
                a.activation(dst, bW[:, P:2 * P].rearrange("p (n a) -> p n a", a=1), ACT.Copy).then_inc(ht_sb, 1)

            pipeline(act, T, [(8, sig_r), (8, sig_z), (5, tanh_score), (6, split_a1), (8, split_a2), (14, split_h1),
                              (8, tanh_n), (3, copy_at), (6, copy_xa), (9, copy_wn), (4, relu_a), (13, relu_b),
                              (14, copy_ht), (16, split_h2)])

            adjb_rows = adjb.rearrange("p t c n -> p (t c) n")

            def next_adj(m, piece):
                first = slice(piece * GB * 3, (piece + 1) * GB * 3)
                if isinstance(m, int):
                    src = adjb_rows[:, first, m * BLK:(m + 1) * BLK]
                else:
                    src = adjb_rows[:, first, bass.ds(m * BLK, BLK)]
                a.activation(ab_s[:, piece * GB:(piece + 1) * GB, :, :].rearrange("p t c i -> p (t c) i"), src,
                             ACT.Copy).then_inc(s_ab, 1)

            act.wait_ge(split_done, T)
            for piece in range(NG):
                next_adj(0, piece)

            def nodes(m, parity, is_last):
                for k in range(BLK):
                    n = m * BLK + k
                    col = slice(k * T, (k + 1) * T)
                    need(act, s_r2p, n + 1)
                    need(act, s_rx, n)
                    a.activation(rg[:, :], r_banks[parity][:, col], ACT.Sigmoid, bias=bias[:, 2:3]).then_inc(s_r2, 1)
                    need(act, s_z2p, n + 1)
                    need(act, s_hcu, n)
                    a.activation(zg[:, :], z_banks[parity][:, col], ACT.Sigmoid, bias=bias[:, 3:4]).then_inc(s_z2, 1)
                    need(act, s_c2p, n + 1)
                    a.activation(hc[:, :], bN[:, col], ACT.Tanh, bias=bias[:, 4:5]).then_inc(s_hc, 1)
                    if k < NG and not is_last:
                        next_adj(m + 1, k)
                    if k == 0 and not (isinstance(m, int) and m == 0):
                        need(act, s_hr, m)
                        a.activation(hntb[:, :, 1, :], hrest[:, :, :], ACT.Copy).then_inc(s_h2, 1)
                if not is_last:
                    need(act, s_dtp2, m + 1)
                    a.activation(dt_s[:, NG // 2:NG, :], bW[:, 0:NG // 2 * P], ACT.Copy).then_inc(s_dts2, 1)
                need(act, s_hscr, 16 * m)
                need(act, s_htp, m + 1)
                a.activation(hnt_s[:, :, :], bN[:, :], ACT.Copy).then_inc(s_hts, 1)
                if not is_last:
                    need(act, s_hrow, 16 * m)
                    need(act, s_hts, m + 1)
                    a.activation(hntb[:, :, 0, :], hnt_s[:, :, :], ACT.Copy).then_inc(s_h1, 1)

            blocks(act, NBLK, nodes)

            def relu2(t, q, u):
                need(act, q_agp, t - UN + 1)
                need(act, q_nm[0], q * 2 + u // 2 + 1)
                a.activation(h2_s[:, u, :], x2_s[:, u, :], ACT.Relu, bias=rs3[:, 0, u, 2:3],
                             scale=rs3[:, 0, u, 1:2]).then_inc(q_h2, 1)

            def copy_agg(t, q, u):
                need(act, q_hip, (t - UN + 1) // 2 if isinstance(t, int) else 2 * q + (u // 2) - 1)
                need(act, q_agp, t + 1)
                a.activation(agg_s[:, u, :], (banks[0], banks[7])[u % 2][:, 0:P], ACT.Copy).then_inc(q_ags, 1)

            def hidden(t, q, u):
                if u % 2 == 0:
                    return
                need(act, q_w2p, t - UN + 1)
                need(act, q_hip, q * 2 + u // 2 + 1)
                for c in range(2):
                    a.activation(hid_s[:, u // 2, c, :], banks[1][:, 2 * c * P:2 * (c + 1) * P], ACT.Relu,
                                 bias=bcol[:, 12 + c:13 + c]).then_inc(q_his, 1)

            def relu3(t, q, u):
                need(act, q_x3h, t - UN + 1)
                need(act, q_n3, t - UN + 1)
                need(act, q_nm[1], q * 2 + u // 2 + 1)
                a.activation(h3_s[:, u, :], x3_s[:, u, :], ACT.Relu, bias=rs3[:, 1, u, 2:3],
                             scale=rs3[:, 1, u, 1:2]).then_inc(q_h3, 1)

            def norm_h3(t, q, u):
                need(act, q_n3p, t - UN + 1)
                need(act, q_nm[2], q * 2 + u // 2 + 1)
                a.activation(n3_s[:, u, :], h3_s[:, u, :], ACT.Identity, bias=rs3[:, 2, u, 2:3],
                             scale=rs3[:, 2, u, 1:2]).then_inc(q_n3, 1)

            def turn_g(t, q, u):
                need(act, q_cvp, t - UN + 1)
                need(act, q_n3p, t + 1)
                a.activation(g3_s[:, u, :], banks[3][:, 0:P], ACT.Identity, bias=bcol[:, 15:16],
                             scale=bcol[:, 14:15]).then_inc(q_g3, 1)

            def copy_y1(t, q, u):
                need(act, q_cvp, t - UN + 1)
                need(act, q_y1p, t + 1)
                a.activation(y1_s[:, u, :], banks[4 + u % 2][:, 0:P], ACT.Copy).then_inc(q_y1, 1)

            pipeline(act, T, [(5, hidden), (4, copy_agg), (15, copy_y1), (14, turn_g), (3, relu2), (10, relu3),
                              (13, norm_h3)])

        @block.vector
        def _(dve):
            v = nc.vector
            dve.wait_ge(s_wload, 16 * NW)
            v.scalar_tensor_tensor(out=junk[:, 0, :], in0=p_bc[:, :], scalar=1.0, in1=p_bc[:, :], op0=ALU.mult,
                                   op1=ALU.mult, accum_out=pn2[:, :]).then_inc(s_setp, 1)
            dve.wait_ge(s_wt_sb, 5)
            v.tensor_tensor(bias[:, 0:2], bcol[:, 0:2], bcol[:, 3:5], ALU.add)
            v.tensor_tensor(bias[:, 2:4], bcol[:, 6:8], bcol[:, 8:10], ALU.add)
            v.tensor_tensor(bias[:, 4:5], bcol[:, 10:11], bcol[:, 11:12], ALU.add).then_inc(s_setp, 1)
            dve.wait_ge(s_const, 8)

            def spread_of(src, st, st_sem):
                def step(t, q, u):
                    v.bn_stats(st[:, u, :], src(t, u)).then_inc(st_sem, 1)
                return step

            def aggregate(st, mv, st_sem, mv_sem):
                def step(t, q, u):
                    need(dve, st_sem, t + 1)
                    if not isinstance(t, int):
                        alone(dve)
                    v.bn_aggr(mv[:, u, :], st[:, u, :]).then_inc(mv_sem, 1)
                return step

            xload = [False]

            def mean_rstd(mv, rs, rs_sem, h_sem, out_sem):
                def step(t, q, u):
                    if u % 2 == 0:
                        return
                    two = slice(u - 1, u + 1)
                    need(dve, h_sem, t - UN + 1)
                    need(dve, rs_sem, pairs(q, u))
                    v.scalar_tensor_tensor(out=rs[:, two, 2:3], in0=mv[:, two, 0:1], scalar=-1.0, in1=rs[:, two, 1:2],
                                           op0=ALU.mult, op1=ALU.mult).then_inc(out_sem, 1)
                return step

            def score_a(t, q, u):
                need(dve, hA, t + 1)
                v.scalar_tensor_tensor(out=junk[:, 0, :], in0=h_a[:, u, :], scalar=1.0, in1=p_bc[:, :], op0=ALU.mult,
                                       op1=ALU.mult, accum_out=score[:, u, :]).then_inc(sc_done, 1)

            def stats_a(t, q, u):
                if isinstance(t, int):
                    dve.wait_ge(s_xload[t >= PRO], 16 if t < PRO else 16 * X_LOADS)
                elif not xload[0]:
                    dve.wait_ge(s_xload[1], 16 * X_LOADS)
                spread_of(lambda t, u: at(x_res, t), st_a, stA)(t, q, u)

            def row_sum(t, q, u):
                need(dve, adj_in[u], 16 * (q + 1))
                v.tensor_reduce(dsum[:, u, 0:1], adj_s[:, u, :], AX_X, ALU.add).then_inc(sum_done, 1)

            def sum2(t, q, u):
                need(dve, sum_done, t + 1)
                v.tensor_scalar(dsum[:, u, 1:2], dsum[:, u, 0:1], 0.0, dsum[:, u, 0:1], ALU.is_equal,
                                ALU.add).then_inc(dv, 1)

            def sum3(t, q, u):
                need(dve, dv, t * 3 + 1)
                v.reciprocal(dsum[:, u, 2:3], dsum[:, u, 1:2]).then_inc(dv, 1)

            def sum4(t, q, u):
                need(dve, dv, t * 3 + 2)
                v.tensor_scalar(dsum[:, u, 3:4], dsum[:, u, 0:1], 0.0, dsum[:, u, 2:3], ALU.not_equal,
                                ALU.mult).then_inc(dv, 1)

            def rank1(t, q, u):
                need(dve, sb_ps, t + 1)
                v.tensor_scalar(junk[:, 1, :], bSB[:, 0:P], score[:, u, :], 0.0, ALU.is_gt, ALU.add,
                                accum_out=cnt[:, u, 0:1])

            def rank1b(t, q, u):
                v.scalar_tensor_tensor(out=junk[:, 2, :], in0=bSB[:, 0:P], scalar=score[:, u, :], in1=below[:, :],
                                       op0=ALU.is_equal, op1=ALU.mult, accum_out=cnt[:, u, 1:2]).then_inc(rk, 1)

            def scale_adj(t, q, u):
                need(dve, s_anout[u], 16 * q)
                need(dve, split_done, t - UN + 1)
                v.tensor_tensor(an_s[:, u, :], adj_s[:, u, :], bSB[:, P:2 * P], ALU.mult).then_inc(adjn_done, 1)

            def rank2(t, q, u):
                need(dve, rk, t * 2 + 1)
                v.tensor_tensor(cnt[:, u, 2:3], cnt[:, u, 0:1], cnt[:, u, 1:2], ALU.add).then_inc(rk, 1)

            def rank3(t, q, u):
                need(dve, xa_ps, t - UN + 1)
                need(dve, th_done, t + 1)
                need(dve, rk, t * 2 + 2)
                v.tensor_scalar(pa_s[:, u, 0, :], iota[:, :], cnt[:, u, 2:3], th[:, u, :], ALU.is_equal,
                                ALU.mult).then_inc(pick_done, 1)

            def gate_n(t, q, u):
                need(dve, n_ps, t + 1)
                need(dve, r_done, t + 1)
                v.scalar_tensor_tensor(out=hn_s[:, :], in0=bN[:, P:2 * P],
                                       scalar=bcol[:, 5:6], in1=r_s[:, :],
                                       op0=ALU.add, op1=ALU.mult).then_inc(hn_done, 1)

            def gate_n2(t, q, u):
                need(dve, hn_done, t + 1)
                v.tensor_tensor(pre_s[:, :], hn_s[:, :], bN[:, 0:P],
                                ALU.add).then_inc(pre_done, 1)

            def new_w(t, q, u):
                need(dve, omz_done, t + 1)
                need(dve, n_done, t + 1)
                v.tensor_tensor(m_s[:, :], omz_s[:, :], n_s[:, :], ALU.mult).then_inc(m_done, 1)

            def new_w2(t, q, u):
                need(dve, zo_done, t + 1)
                need(dve, wt_ps, t - 1)
                need(dve, m_done, t + 1)
                v.tensor_tensor(w_s[:, (u + 1) % 2, :], m_s[:, :], zw_s[:, :], ALU.add).then_inc(w_ready, 1)

            def x1(t, q, u):
                need(dve, out_ps, t + 1)
                v.tensor_tensor(at(x_res, t), at(x_res, t), bO[:, 0:P], ALU.add).then_inc(x1_done, 1)

            def stats_b(t, q, u):
                need(dve, x1_done, t + 1)
                if not isinstance(t, int):
                    alone(dve)
                spread_of(lambda t, u: at(x_res, t), st_b, stB)(t, q, u)

            pipeline(dve, T, [(8, gate_n), (4, sum2), (8, gate_n2), (5, rank1), (5, rank1b), (8, new_w),
                              (3, mean_rstd(mv_a, rs_a, rsA, hA, nmA)), (4, sum3),
                              (12, mean_rstd(mv_b, rs_b, rsB, hB, nmB)), (8, new_w2),
                              (5, scale_adj), (5, rank2), (10, x1), (1, stats_a), (4, sum4), (5, rank3),
                              (10, stats_b), (1, aggregate(st_a, mv_a, stA, mvA)), (4, score_a), (3, row_sum),
                              (10, aggregate(st_b, mv_b, stB, mvB))])

            dve.wait_ge(s_ctp, 1)
            v.tensor_copy(cf_turned, bO[:, :]).then_inc(s_cts, 1)

            def grouped(ap):
                return ap.rearrange("p (b g) -> p g b", g=NG)

            def nodes(m, parity, is_last):
                done = [0]

                def count(ins):
                    done[0] += 1
                    ins.then_inc(s_v, 1)
                    return done[0]

                def after(n):
                    need(dve, s_v, m * VS + n)

                need(dve, s_xp, m + 1)
                xp_bank = bAT[:, :].rearrange("p (b i) -> p i b", i=BLK)
                v.tensor_copy(xp_s[:, 0:1, :], xp_bank[:, 0:1, :]).then_inc(s_xpr, 1)
                x_ready = count(v.tensor_copy(xp_s[:, 1:BLK, :], xp_bank[:, 1:BLK, :]))
                need(dve, s_cf, 16 * (BLK - 1) * (m + 1))
                for k in range(BLK):
                    n = m * BLK + k
                    s2 = k % 2
                    h_in = h_t[:, n, :] if isinstance(m, int) else \
                        h_t[:, bass.ds(n, 1), :].rearrange("p a b -> p (a b)")
                    need(dve, s_xpr, n + 1)
                    need(dve, s_r2, n + 1)
                    v.tensor_tensor(rx[:, :], rg[:, :], xp_s[:, k, :], ALU.mult).then_inc(s_rx, 1)
                    need(dve, s_z2, n + 1)
                    c_zx = count(v.tensor_tensor(zx[:, s2, :], zg[:, :], xp_s[:, k, :], ALU.mult))
                    v.tensor_scalar(omz2[:, s2, :], zg[:, :], -1.0, 1.0, ALU.mult, ALU.add).then_inc(s_hcu, 1)
                    after(c_zx)
                    c_u = count(v.tensor_tensor(zxh[:, s2, :], zx[:, s2, :], h_in, ALU.subtract))
                    if k < BLK - 1:
                        need(dve, s_hcu, n + 1)
                        c_b = count(v.tensor_tensor(c_omz[:, s2, :], cf(k, k + 1), omz2[:, s2, :], ALU.mult))
                        after(c_u)
                        c_cu = count(v.tensor_tensor(c_zxh[:, s2, :], cf(k, k + 1), zxh[:, s2, :], ALU.mult))
                        after(max(c_cu, x_ready))
                        c_a = count(v.tensor_tensor(xp_a[:, s2, :], xp_s[:, k + 1, :], c_zxh[:, s2, :], ALU.add))
                        need(dve, s_hc, n + 1)
                        after(c_b)
                        c_p = count(v.tensor_tensor(p1[:, s2, :], c_omz[:, s2, :], hc[:, :], ALU.mult))
                        c_t = count(v.tensor_tensor(t1[:, s2, :], omz2[:, s2, :], hc[:, :], ALU.mult))
                        after(max(c_p, c_a))
                        v.tensor_tensor(xp_s[:, k + 1, :], xp_a[:, s2, :], p1[:, s2, :], ALU.add).then_inc(s_xpr, 1)
                    else:
                        need(dve, s_hcu, n + 1)
                        need(dve, s_hc, n + 1)
                        c_t = count(v.tensor_tensor(t1[:, s2, :], omz2[:, s2, :], hc[:, :], ALU.mult))
                    if k == 0:
                        need(dve, s_dtp2, m)
                        need(dve, s_htp, m)
                    after(max(c_t, c_u))
                    change = v.tensor_tensor(dl_s[:, :, k, :], grouped(t1[:, s2, :]), grouped(zxh[:, s2, :]), ALU.add)
                    if k < BLK - 1:
                        c_dl = count(change)
                    else:
                        change.then_inc(s_dl, 1)
                    state = v.tensor_tensor(hn2[:, :, k, :], grouped(t1[:, s2, :]), grouped(zx[:, s2, :]), ALU.add)
                    if k < BLK - 1:
                        count(state)
                    else:
                        state.then_inc(s_hn, 1)
                    rest = BLK - 2 - k
                    if rest > 0:
                        after(c_dl)
                        wide = dl_s[:, :, k, :].rearrange("p g (a b) -> p a g b", a=1).to_broadcast([P, rest, NG, GB])
                        o = cf_first[k] + T
                        c_p2 = count(v.tensor_tensor(
                            p2[:, 0:rest, :].rearrange("p i (b g) -> p i g b", g=NG),
                            cf_flat[:, o:o + rest * T].rearrange("p (i b g) -> p i g b", b=GB, g=NG), wide, ALU.mult))
                        after(c_p2)
                        dve.sem_inc(s_cfu, 1)
                        x_ready = count(v.tensor_tensor(xp_s[:, k + 2:BLK, :], xp_s[:, k + 2:BLK, :],
                                                        p2[:, 0:rest, :], ALU.add))
                    elif rest == 0:
                        after(c_dl)
                        dve.sem_inc(s_cfu, 1)
                if not is_last:
                    need(dve, s_dtp, m + 1)
                    v.tensor_copy(dt_s[:, 0:NG // 2, :], bO[:, 0:NG // 2 * P]).then_inc(s_dts, 1)
                assert done[0] < VS
                dve.sem_inc(s_v, VS - done[0])

            blocks(dve, NBLK, nodes)

            dve.wait_ge(s_xp, NBLK)
            dve.wait_ge(s_wload3, 16 * NW3)
            v.tensor_scalar(eps1[:, :], eps1[:, :], 1.0, None, ALU.add).then_inc(s_setp, 1)
            dve.wait_ge(s_setp, 3)
            v.tensor_scalar(eye_eps[:, :], ident[:, :], eps1[:, 0:1], None, ALU.mult).then_inc(s_setp, 1)

            def x2(t, q, u):
                need(dve, q_x2b, t - UN + 1)
                need(dve, q_h2, t - UN + 1)
                need(dve, in_ld[u], 48 * (q + 1))
                v.tensor_tensor(x2_s[:, u, :], at(x_res, t), h_in[:, u, :], ALU.add).then_inc(q_x2, 1)

            def x3(t, q, u):
                need(dve, q_x3h, t - UN + 1)
                need(dve, q_h3, t - UN + 1)
                need(dve, q_x2b, t + 1)
                need(dve, q_w2p, t + 1)
                v.tensor_tensor(x3_s[:, u, :], at(x_res, t), (banks[2], banks[6])[u % 2][:, 0:P],
                                ALU.add).then_inc(q_x3, 1)

            def spread3(i, src, ready):
                def step(t, q, u):
                    need(dve, ready, t + 1)
                    v.bn_stats(st3[:, i, u, :], src[:, u, :]).then_inc(q_st[i], 1)
                return step

            def aggregate3(i):
                return aggregate(st3[:, i, :, :], mv3[:, i, :, :], q_st[i], q_mv[i])

            def finish_a(t, q, u):
                need(dve, q_cvp, t + 1)
                v.tensor_tensor(cb_s[:, u, :], banks[4 + u % 2][:, P:2 * P], brel_bc[:, :], ALU.add).then_inc(q_cb, 1)

            def finish_b(t, q, u):
                need(dve, o_st[u], 16 * q)
                need(dve, q_x3h, t + 1)
                need(dve, q_cb, t + 1)
                v.scalar_tensor_tensor(out=o_s[:, u, :], in0=cb_s[:, u, :], scalar=0.0, in1=at(x_res, t),
                                       op0=ALU.max, op1=ALU.add).then_inc(q_o, 1)

            def x3h(t, q, u):
                need(dve, q_h3, t + 1)
                v.tensor_tensor(at(x_res, t), x3_s[:, u, :], h3_s[:, u, :], ALU.add).then_inc(q_x3h, 1)

            def nm3(i, h_sem):
                return mean_rstd(mv3[:, i, :, :], rs3[:, i, :, :], q_rs[i], h_sem, q_nm[i])

            pipeline(dve, T, [(1, x2), (8, x3), (11, x3h), (1, spread3(0, x2_s, q_x2)), (2, nm3(0, q_h2)), (9, nm3(1, q_h3)),
                              (12, nm3(2, q_n3)), (11, spread3(2, h3_s, q_h3)), (16, finish_a),
                              (8, spread3(1, x3_s, q_x3)), (1, aggregate3(0)), (11, aggregate3(2)), (16, finish_b),
                              (8, aggregate3(1))])

        @block.tensor
        def _(pe):
            mm, turn = nc.tensor.matmul, nc.tensor.transpose
            pe.wait_ge(s_wload, 16 * NW)
            pe.wait_ge(s_const, 8)
            for i in range(13):
                ins = turn(banks[i // 4][:, (i % 4) * P:(i % 4 + 1) * P], w_nat[:, i, :], ident[:, :])
                if i % 4 == 3:
                    ins.then_inc(s_wt_ps, 1)
            turn(banks[3][:, P:P + 16], b_nat[:, :], ident[0:16, 0:16]).then_inc(s_wt_ps, 1)
            pe.wait_ge(s_wt_sb, 5)

            def add(out_, l, r, start=False):
                return mm(out_, l, r, start=start, stop=True, skip_group_check=True)

            def turn_adj(t, q, u):
                need(pe, at_sb, t)
                need(pe, adj_in[u], 16 * (q + 1))
                turn(bAT[:, 0:P], adj_s[:, u, :], ident[:, :]).then_inc(at_ps, 1)

            def spread(t, q, u):
                need(pe, adjn_done, t)
                need(pe, sc_done, t + 1)
                need(pe, dv, t * 3 + 3)
                turn(bSB[:, 0:P], score[:, u, :].to_broadcast([P, P]), ident[:, :])
                turn(bSB[:, P:2 * P], dsum[:, u, 3:4].to_broadcast([P, P]), ident[:, :]).then_inc(sb_ps, 1)

            def pick_rows(t, q, u):
                need(pe, xa_sb, t)
                need(pe, hA, t + 1)
                need(pe, at_sb, t + 1)
                need(pe, pick_done, t + 1)
                mm(bXA[:, 0:2 * P], h_a[:, u, :], pa_s[:, u, :, :].rearrange("p c n -> p (c n)"),
                   start=True, stop=True).then_inc(xa_ps, 1)

            def gru_in(t, q, u):
                need(pe, xa_sb, t + 1)
                for bank, done, w in ((bR, r_done, W_IH), (bZ, z_done, W_IH + 1), (bN, pre_done, W_IH + 2)):
                    need(pe, done, t)
                    add(bank[:, 0:P], w_t[:, w, :], xa_s[:, u, 0:P], True)

            def gru_state(t, q, u):
                need(pe, w_ready, t + 1)
                add(bR[:, 0:P], w_t[:, W_HH, :], w_s[:, u % 2, :]).then_inc(r_ps, 1)
                add(bN[:, P:2 * P], w_t[:, W_HH + 2, :], w_s[:, u % 2, :]).then_inc(n_ps, 1)
                add(bZ[:, 0:P], w_t[:, W_HH + 1, :], w_s[:, u % 2, :]).then_inc(z_ps, 1)

            def turn_w(t, q, u):
                need(pe, wn_sb, t)
                need(pe, ht_sb, t - 5)
                need(pe, w_ready, t + 2)
                turn(bW[:, 0:P], w_s[:, (u + 1) % 2, :], ident[:, :]).then_inc(wt_ps, 1)

            def layer0(t, q, u):
                need(pe, x1_done, t)
                need(pe, wn_sb, t + 1)
                mm(bO[:, 0:P], xa_s[:, u, P:2 * P], wn_s[:, u % 2, :], start=True, stop=True).then_inc(out_ps, 1)

            def turn_h(t, q, u):
                need(pe, ht_sb, t)
                need(pe, wn_sb, min(t + 5, T) if isinstance(t, int) else t + 5)
                need(pe, hB, t + 1)
                turn(bW[:, P:2 * P], h_b[:, u, :], ident[:, :]).then_inc(ht_ps, 1)

            pipeline(pe, T, [(8, gru_state), (10, layer0), (6, pick_rows), (5, spread), (14, turn_h), (9, turn_w),
                             (3, turn_adj), (7, gru_in)])

            TERMS = ((0, 0), (0, 1), (1, 0), (0, 2), (1, 1), (2, 0))

            def gather(m, graphs):
                for b in graphs:
                    for i, (c, e) in enumerate(TERMS):
                        if b % GB == 0 and i == 0:
                            need(pe, s_ab, m * NG + b // GB + 1)
                        ins = add(bAT[:, b * BLK:(b + 1) * BLK], hb[:, b, c, :], ab_s[:, b, e, :], b == 0 and i == 0)
                return ins

            def own_part(bank, read, w, m, count, nodes=range(BLK)):
                first = nodes[0]
                if first == 0:
                    need(pe, read, count)
                if isinstance(m, int):
                    src = h_t[:, m * BLK + first:m * BLK + first + len(nodes), :]
                else:
                    if first == 0:
                        alone(pe)
                    src = h_t[:, bass.ds(m * BLK + first, len(nodes)), :]
                add(bank[:, first * T:(first + len(nodes)) * T], w_t[:, w, :], src.rearrange("p n b -> p (n b)"),
                    first == 0)

            pe.wait_ge(ht_sb, T)
            pe.wait_ge(x1_done, T)
            pe.wait_ge(at_sb, T)
            own_part(bR, s_r2, W_IX, 0, 0)
            own_part(bZ, s_z2, W_IX + 1, 0, 0)
            own_part(bN, s_hc, W_CX, 0, 0)

            pe.wait_ge(s_coef, 16 * BLK)
            coef_rows = coef[:, :, :, :].rearrange("b m j i -> b (m j i)")
            for c in range(NBLK // 2):
                ins = turn(bO[:, c * T:(c + 1) * T], coef_rows[:, c * P:(c + 1) * P], ident[0:T, 0:T])
            ins.then_inc(s_ctp, 1)

            pe.wait_ge(hnat, T)
            pe.wait_ge(split_done, T)
            gather(0, range(T)).then_inc(s_xp, 1)

            def nodes(m, parity, is_last):
                share = [0, 0, 10, 11, 11, 11, 11, 10]
                b0 = 0
                for k in range(BLK):
                    n = m * BLK + k
                    col = slice(k * T, (k + 1) * T)
                    todo = list(range(b0, b0 + share[k])) if not is_last else []
                    b0 += share[k]
                    need(pe, s_xpr, n + 1)
                    add(r_banks[parity][:, col], w_t[:, W_IH1, :], xp_s[:, k, :]).then_inc(s_r2p, 1)
                    add(z_banks[parity][:, col], w_t[:, W_IH1 + 1, :], xp_s[:, k, :]).then_inc(s_z2p, 1)
                    early = 4 if todo else 0
                    if todo:
                        if k == 2:
                            need(pe, s_v, m * VS + 1)
                            need(pe, s_hrow, 16 * m)
                        gather(m + 1, todo[:early])
                    if k == 0 and not (isinstance(m, int) and m == 0):
                        own_part(bN, s_hts, W_CX, m, m, range(2, BLK))
                    own = None
                    if k < 2 and not is_last:
                        own = ((r_banks[1 - parity], s_r2, W_IX, m + 1, m * BLK),
                               (z_banks[1 - parity], s_z2, W_IX + 1, m + 1, m * BLK))[k]
                        if k == 1:
                            own_part(*own, range(0, 2))
                    need(pe, s_rx, n + 1)
                    add(bN[:, col], w_t[:, W_CH, :], rx[:, :]).then_inc(s_c2p, 1)
                    if own:
                        own_part(*own, range(2 * k, BLK))
                    if todo:
                        gather(m + 1, todo[early:])
                assert b0 == T, b0
                if not is_last:
                    need(pe, s_dts, m)
                    need(pe, s_dts2, m)
                    need(pe, s_dl, m + 1)
                    for g in range(NG):
                        bank, c = (bO, bW)[g // 2], g % 2 * P
                        ins = turn(bank[:, c:c + P], dl_s[:, g, :, :].rearrange("p k b -> p (k b)"), ident[:, :])
                        if g == NG // 2 - 1:
                            ins.then_inc(s_dtp, 1)
                    ins.then_inc(s_dtp2, 1)

                def turn_states(groups):
                    for g in groups:
                        ins = turn(bN[:, g * P:(g + 1) * P], hn2[:, g, :, :].rearrange("p k b -> p (k b)"), ident[:, :])
                    return ins

                need(pe, s_hn, m + 1)
                if not is_last:
                    turn_states(range(NG)).then_inc(s_htp, 1)
                    need(pe, s_bd, m + 1)
                    for g in range(NG):
                        if g % 2 == 0:
                            need(pe, (s_dts, s_dts2)[g // 2], m + 1)
                        ins = add(bAT[:, :].rearrange("p (b g i) -> p g b i", g=NG, i=BLK)[:, g, :, :], dt_s[:, g, :],
                                  bd_s[:, g, :, :])
                    ins.then_inc(s_xp, 1)
                    own_part(bN, s_hts, W_CX, m + 1, m + 1, range(0, 2))
                else:
                    turn_states(range(NG)).then_inc(s_htp, 1)

            blocks(pe, NBLK, nodes)

            pe.wait_ge(s_hts, NBLK)
            pe.wait_ge(s_wload3, 16 * NW3)

            def aggregate(t, q, u):
                need(pe, q_ags, t - 1)
                need(pe, q_h2, t + 1)
                need(pe, q_ae, t + 1)
                mm((banks[0], banks[7])[u % 2][:, 0:P], h2_s[:, u, :], ae_s[:, u, :], start=True,
                   stop=True).then_inc(q_agp, 1)

            def mlp_in(t, q, u):
                if u % 2 == 0:
                    return
                need(pe, q_his, t - 1)
                need(pe, q_ags, t + 1)
                two = agg_s[:, u - 1:u + 1, :].rearrange("p a n -> p (a n)")
                mm(banks[1][:, 0:2 * P], w1[:, 0, :], two, start=True, stop=True)
                mm(banks[1][:, 2 * P:4 * P], w1[:, 1, :], two, start=True, stop=True).then_inc(q_hip, 1)

            def mlp_out(t, q, u):
                need(pe, q_x3, t - 1)
                need(pe, q_his, 4 * q + 2 * (u // 2) + 2)
                bank = (banks[2], banks[6])[u % 2]
                col = slice((u % 2) * P, (u % 2 + 1) * P)
                mm(bank[:, 0:P], hid_s[:, u // 2, 0, col], w2[:, 0, :], start=True, stop=False)
                mm(bank[:, 0:P], hid_s[:, u // 2, 1, col], w2[:, 1, :], start=False, stop=True).then_inc(q_w2p, 1)

            def turn_n3(t, q, u):
                need(pe, q_g3, t)
                need(pe, q_n3, t + 1)
                turn(banks[3][:, 0:P], n3_s[:, u, :], ident[:, :]).then_inc(q_n3p, 1)

            def rel_root(t, q, u):
                need(pe, q_cb, t - 1)
                need(pe, q_g3, t + 1)
                add(banks[4 + u % 2][:, 0:2 * P], g3_s[:, u, :], wrr[:, :, :].rearrange("p c n -> p (c n)"),
                    True).then_inc(q_y1p, 1)

            def conv(t, q, u):
                need(pe, q_y1, t + 1)
                need(pe, ac_ld[u], 16 * (q + 1))
                add(banks[4 + u % 2][:, P:2 * P], ac_in[:, u, :], y1_s[:, u, :]).then_inc(q_cvp, 1)

            pipeline(pe, T, [(5, mlp_in), (8, mlp_out), (4, aggregate), (15, rel_root), (14, turn_n3), (16, conv)])


_INS = ['x', 'adj', 'L0_gnn_pool_p', 'L0_gnn_W_ih', 'L0_gnn_W_hh', 'L0_gnn_b_ih', 'L0_gnn_b_hh', 'L0_gnn_W0',
        'L1_gnn_W_ioux', 'L1_gnn_b_ioux', 'L1_gnn_W_iouh', 'L1_gnn_b_iouh', 'L1_gnn_W_coux', 'L1_gnn_b_coux',
        'L1_gnn_W_couh', 'L1_gnn_b_couh', 'L2_gnn_eps', 'L2_gnn_W1', 'L2_gnn_b1', 'L2_gnn_W2', 'L2_gnn_b2',
        'L3_gnn_W_rel', 'L3_gnn_b_rel', 'L3_gnn_W_root', 'L3_gnn_ln_gamma', 'L3_gnn_ln_beta']


def kernel(**inputs):
    import numpy as _np
    import concourse.bacc as _bacc
    from concourse import mybir as _mybir
    from concourse.bass_utils import run_bass_kernel_spmd as _run

    nc = _bacc.Bacc("TRN2", target_bir_lowering=False, num_devices=1)
    arrays, dram = {}, {}
    for name in _INS:
        a = _np.ascontiguousarray(inputs[name])
        arrays[f"in_{name}_dram"] = a
        dram[name] = nc.dram_tensor(f"in_{name}_dram", a.shape, _mybir.dt.from_np(a.dtype), kind="ExternalInput").ap()
    out = nc.dram_tensor("out_0_dram", inputs["x"].shape, _mybir.dt.float32, kind="ExternalOutput").ap()
    graph_layers(nc, dram, out)
    r = _run(nc, [arrays], core_ids=[0])
    return r.results[0]["out_0_dram"]
```
